# Optimizing a Trainium2 kernel written in Bass

```python
import numpy as np
import jax
import jax.numpy as jnp

def _softmax(x, axis=-1):
    return jax.nn.softmax(x, axis=axis)

def _gelu(x):
    return jax.nn.gelu(x, approximate=True)

def _silu(x):
    return jax.nn.silu(x)

def _sigmoid(x):
    return jax.nn.sigmoid(x)

def _layernorm(x, axis=-1, eps=1e-05):
    m = jnp.mean(x, axis=axis, keepdims=True)
    v = jnp.var(x, axis=axis, keepdims=True)
    return (x - m) / jnp.sqrt(v + eps)

def _scatter_add(tgt, idx, src, axis=0):
    return tgt.at[idx].add(src)

def _segment_sum(src, seg, n):
    return jax.ops.segment_sum(src, seg, n)
kernel_name = 'mk_adj_resnorm_d4_adj_r2_5634e0'

def setup_inputs(seed: int=0):
    np.random.seed(seed)
    _w = jnp.asarray

    def _rec_inputs():
        import jax
        import jax.numpy as jnp
        _gk = jax.random.key(seed)
        x = -0.0002928 + 1 * jax.random.normal(jax.random.fold_in(_gk, 1), (32, 256, 128), jnp.float32)
        _a = jax.random.bernoulli(jax.random.fold_in(_gk, 2), 0.015625, (32, 256, 256))
        _a = jnp.logical_or(_a, jnp.swapaxes(_a, -1, -2))
        _a = jnp.logical_or(_a, jnp.eye(256, dtype=bool))
        adj = _a.astype(jnp.int32)
        return (x, adj)
    x, adj = _rec_inputs()

    def _L0_gnn_setup():
        import jax, jax.numpy as jnp
        import numpy as np
        NEG_INF = -1000000000.0
        LEAKY_SLOPE = 0.2
        key = jax.random.key(seed)
        k1, k2, k3, k4, k5 = jax.random.split(key, 5)
        B, N, F_in, F_out = (8, 1024, 128, 128)
        x = jax.random.normal(k1, (B, N, F_in), dtype=jnp.float32)
        adj = jax.random.randint(k2, (B, N, N), 0, 2, dtype=jnp.int32)
        W = jax.random.normal(k3, (F_out, F_in), dtype=jnp.float32) * 0.05
        a_src = jax.random.normal(k4, (F_out,), dtype=jnp.float32) * 0.05
        a_dst = jax.random.normal(k5, (F_out,), dtype=jnp.float32) * 0.05
        return {'x': x, 'adj': adj, 'W': W, 'a_src': a_src, 'a_dst': a_dst}
    _L0_gnn_all = _L0_gnn_setup()
    _L0_gnn_in = {k: v for k, v in _L0_gnn_all.items() if k in ('W', 'a_src', 'a_dst')}
    del _L0_gnn_all

    def _L1_gnn_setup():
        import jax, jax.numpy as jnp
        import numpy as np
        NEG_INF = -9000000000000000.0
        ALPHA = 0.2
        key = jax.random.key(seed)
        k1, k2, k3, k4 = jax.random.split(key, 4)
        B, N, Fin, Fout = (8, 1024, 128, 128)
        h = jax.random.normal(k1, (B, N, Fin), dtype=jnp.float32)
        adj = jax.random.randint(k2, (B, N, N), 0, 2, dtype=jnp.int32)
        W = jax.random.normal(k3, (Fout, Fin), dtype=jnp.float32) / np.sqrt(Fin)
        a = jax.random.normal(k4, (2 * Fout,), dtype=jnp.float32) / np.sqrt(2 * Fout)
        return {'h': h, 'adj': adj, 'W': W, 'a': a}
    _L1_gnn_all = _L1_gnn_setup()
    _L1_gnn_in = {k: v for k, v in _L1_gnn_all.items() if k in ('W', 'a')}
    del _L1_gnn_all

    def _L2_gnn_setup():
        import jax, jax.numpy as jnp
        import numpy as np
        B, S, D = (64, 256, 128)

        def _leaky(x):
            return jnp.where(x >= 0, x, 0.2 * x)
        key = jax.random.key(seed)
        k = jax.random.split(key, 6)
        stdv = 1.0 / np.sqrt(D)
        return {'hidden': jax.random.normal(k[0], (B, S, D), dtype=jnp.float32), 'adj': jax.random.randint(k[1], (B, S, S), 0, 5, dtype=jnp.int32), 'a0': jax.random.uniform(k[2], (D, 1), jnp.float32, -stdv, stdv), 'a1': jax.random.uniform(k[3], (D, 1), jnp.float32, -stdv, stdv), 'a2': jax.random.uniform(k[4], (D, 1), jnp.float32, -stdv, stdv), 'a3': jax.random.uniform(k[5], (D, 1), jnp.float32, -stdv, stdv), 'bias': jnp.zeros((D,), dtype=jnp.float32)}
    _L2_gnn_all = _L2_gnn_setup()
    _L2_gnn_in = {k: v for k, v in _L2_gnn_all.items() if k in ('a0', 'a1', 'a2', 'a3', 'bias')}
    del _L2_gnn_all

    def _L3_gnn_setup():
        import jax, jax.numpy as jnp
        import numpy as np
        B, N, D_IN, D_OUT, R = (8, 1024, 128, 128, 4)
        key = jax.random.key(seed)
        k1, k2, k3, k4 = jax.random.split(key, 4)
        x = jax.random.normal(k1, (B, N, D_IN), dtype=jnp.float32)
        adj = jnp.zeros((1,), dtype=jnp.float32)
        relation = jax.random.randint(k2, (B, N, N), 0, R + 1, dtype=jnp.int32)
        weight = jax.random.normal(k3, (R, D_IN, D_OUT), dtype=jnp.float32) * 0.05
        bias = jax.random.normal(k4, (D_OUT,), dtype=jnp.float32) * 0.05
        return {'x': x, 'adj': adj, 'relation': relation, 'weight': weight, 'bias': bias}
    _L3_gnn_all = _L3_gnn_setup()
    _L3_gnn_in = {k: v for k, v in _L3_gnn_all.items() if k in ('adj', 'weight', 'bias')}
    del _L3_gnn_all
    return {'x': x, 'adj': adj, 'L0_gnn_W': _L0_gnn_in['W'], 'L0_gnn_a_src': _L0_gnn_in['a_src'], 'L0_gnn_a_dst': _L0_gnn_in['a_dst'], 'L1_gnn_W': _L1_gnn_in['W'], 'L1_gnn_a': _L1_gnn_in['a'], 'L2_gnn_a0': _L2_gnn_in['a0'], 'L2_gnn_a1': _L2_gnn_in['a1'], 'L2_gnn_a2': _L2_gnn_in['a2'], 'L2_gnn_a3': _L2_gnn_in['a3'], 'L2_gnn_bias': _L2_gnn_in['bias'], 'L3_gnn_adj': _L3_gnn_in['adj'], 'L3_gnn_weight': _L3_gnn_in['weight'], 'L3_gnn_bias': _L3_gnn_in['bias']}

def reference(x, adj, L0_gnn_W, L0_gnn_a_src, L0_gnn_a_dst, L1_gnn_W, L1_gnn_a, L2_gnn_a0, L2_gnn_a1, L2_gnn_a2, L2_gnn_a3, L2_gnn_bias, L3_gnn_adj, L3_gnn_weight, L3_gnn_bias):
    import jax
    import jax.numpy as jnp

    def _L0_gnn_ref(x, adj, W, a_src, a_dst):
        import jax, jax.numpy as jnp
        import numpy as np
        NEG_INF = -1000000000.0
        LEAKY_SLOPE = 0.2
        h = jnp.einsum('bnf,of->bno', x, W)
        s_src = h @ a_src
        s_dst = h @ a_dst
        e = s_src[:, :, None] + s_dst[:, None, :]
        e = jax.nn.leaky_relu(e, negative_slope=LEAKY_SLOPE)
        e = jnp.where(adj == 0, jnp.float32(NEG_INF), e)
        alpha = jax.nn.softmax(e, axis=-1)
        h_prime = jnp.einsum('bij,bjo->bio', alpha, h)
        return h_prime

    def _L1_gnn_ref(h, adj, W, a):
        import jax, jax.numpy as jnp
        import numpy as np
        NEG_INF = -9000000000000000.0
        ALPHA = 0.2
        Wh = jnp.einsum('bnf,of->bno', h, W)
        Fout = Wh.shape[-1]
        a1, a2 = (a[:Fout], a[Fout:])
        f_i = Wh @ a1
        f_j = Wh @ a2
        e = f_i[:, :, None] + f_j[:, None, :]
        e = jnp.where(e > 0, e, ALPHA * e)
        e = jnp.where(adj == 0, NEG_INF, e)
        attention = jax.nn.softmax(e, axis=2)
        h_prime = jnp.einsum('bij,bjo->bio', attention, Wh)
        return h_prime

    def _L2_gnn_ref(hidden, adj, a0, a1, a2, a3, bias):
        import jax, jax.numpy as jnp
        import numpy as np
        B, S, D = (64, 256, 128)

        def _leaky(x):
            return jnp.where(x >= 0, x, 0.2 * x)
        h = hidden

        def e_of(a):
            return _leaky(jnp.einsum('bid,bjd->bij', h * a[:, 0], h))
        e0, e1, e2, e3 = (e_of(a0), e_of(a1), e_of(a2), e_of(a3))
        neg_inf = jnp.float32(-jnp.finfo(e0.dtype).max)
        alpha = jnp.where(adj == 1, e0, neg_inf)
        alpha = jnp.where(adj == 2, e1, alpha)
        alpha = jnp.where(adj == 3, e2, alpha)
        alpha = jnp.where(adj == 4, e3, alpha)
        alpha = jax.nn.sigmoid(alpha)
        return jnp.einsum('bij,bjd->bid', alpha, h) + bias

    def _L3_gnn_ref(x, adj, relation, weight, bias):
        import jax, jax.numpy as jnp
        import numpy as np
        B, N, D_IN, D_OUT, R = (8, 1024, 128, 128, 4)
        rel_ids = jnp.arange(1, weight.shape[0] + 1, dtype=relation.dtype)
        masks = (relation[None] == rel_ids[:, None, None, None]).astype(x.dtype)
        h = jnp.einsum('rbnm,bmd->rbnd', masks, x)
        y = jnp.einsum('rbnd,rdo->bno', h, weight)
        return y + bias
    x = _layernorm(x + _L0_gnn_ref(x, adj, L0_gnn_W, L0_gnn_a_src, L0_gnn_a_dst), axis=-1)
    x = _layernorm(x + _L1_gnn_ref(x, adj, L1_gnn_W, L1_gnn_a), axis=-1)
    x = _layernorm(x + _L2_gnn_ref(x, adj, L2_gnn_a0, L2_gnn_a1, L2_gnn_a2, L2_gnn_a3, L2_gnn_bias), axis=-1)
    x = _layernorm(x + _L3_gnn_ref(x, L3_gnn_adj, adj, L3_gnn_weight, L3_gnn_bias), axis=-1)
    return x

_drawn_inputs = setup_inputs


def setup_inputs(seed=0):
    import zlib

    import numpy as np

    out = dict(_drawn_inputs(seed))
    spreads = {'L2_gnn_bias': (0.0, 0.1)}
    factors = {'L0_gnn_a_src': 4.144, 'L3_gnn_bias': 4.021}
    for name, (base, spread) in spreads.items():
        noise = np.random.default_rng([zlib.crc32(name.encode()), seed]).standard_normal(out[name].shape)
        drawn = base * np.exp(spread * noise) if base else spread * noise
        out[name] = jnp.asarray(drawn.astype(out[name].dtype))
    for name, factor in factors.items():
        out[name] = (out[name] * factor).astype(out[name].dtype)
    return out
```

```python
from contextlib import ExitStack

import concourse.bass as bass
from concourse import mybir

P = 128
SLOPE = 0.2
EPS = 1e-5
ALU = mybir.AluOpType
ACT = mybir.ActivationFunctionType
AX = mybir.AxisListType
F32 = mybir.dt.float32
BF16 = mybir.dt.bfloat16
I32 = mybir.dt.int32

GEN_PE = ["adjT"]
for _l in "01":
    GEN_PE += [n + _l for n in ("xT", "h", "dst", "pT", "out")]
GEN_PE += ["xT2"] + [f"score{r}" for r in range(4)] + ["out2", "xT3", "xw", "out3"]
GEN_ACT = ["adjT"]
for _l in "01":
    GEN_ACT += [n + _l for n in ("xT", "h", "sum", "exp", "pT")]
GEN_ACT += ["xT2"]
for _r in "0123":
    GEN_ACT += ["score" + _r, "sigmoid" + _r]
GEN_ACT += ["xT3", "xw"]
LN_STEPS = ["res", "stats", "aggr", "var", "norm"]
GEN_DVE = ["adj", "edge", "none0", "none1"]
for _l in "01":
    GEN_DVE += [n + _l for n in ("leaky", "keep", "mask", "max", "negmax", "rinv")] + [n + _l for n in LN_STEPS]
GEN_DVE += ["xTa"]
for _r in "0123":
    GEN_DVE += ["leaky2" + _r, "pick" + _r] + (["sum" + _r] if _r != "0" else [])
GEN_DVE += ["add2"] + [n + "2" for n in LN_STEPS] + ["rel3", "add3"] + [n + "3" for n in LN_STEPS]
GEN_POOL = [f"pow{l}" for l in range(4)]


def done(steps, g, name):
    return g * len(steps) + steps.index(name) + 1


def res_gnn_kernel(nc, x, adj, W0, a_src0, a_dst0, W1, a1, a2_0, a2_1, a2_2, a2_3, bias2, adj3, W3, bias3, out):
    B, N, D = x.shape
    NB = N // P
    R = W3.shape[0]
    assert D == P and NB == 2 and R == 4
    HC = D + 2

    x_blocks = x.rearrange("g (b p) d -> g p b d", p=P)
    out_blocks = out.rearrange("g (b p) d -> g p b d", p=P)
    adj_blocks = adj.rearrange("g (b p) n -> g p b n", p=P)

    with ExitStack() as ctx:
        def sb(name, shape, dt=F32):
            return ctx.enter_context(nc.sbuf_tensor(name, shape, dt))

        def bank(name, shape, dt=F32):
            return ctx.enter_context(nc.psum_tensor(name, shape, dt))

        def sem(name):
            return ctx.enter_context(nc.semaphore(name))

        zero = sb("zero", [P, P])
        ident = sb("ident", [P, P])
        ident_bf = sb("ident_bf", [P, P], BF16)
        minus_half = sb("minus_half", [P, NB])
        w_nat = sb("w_nat", [P, 2, D])
        a_col = sb("a_col", [P, 2, 2])
        a_rep = sb("a_rep", [P, 2, P])
        w_ext = sb("w_ext", [P, 2, HC])
        wd_rep = sb("wd_rep", [P, 2, P])
        a2 = sb("a2", [P, 4])
        w3 = sb("w3", [P, R, D])
        bias = sb("bias", [P, 2, NB, D])

        xg = sb("xg", [P, NB, D])
        adj_i = sb("adj_i", [P, NB, N], I32)
        adj_bf = sb("adj_bf", [P, NB, N], BF16)
        adjT = sb("adjT", [P, NB, N], BF16)
        edge = sb("edge", [P, NB, N])
        none = sb("none", [P, 2, NB, N])
        xT = sb("xT", [P, N])
        xTa = sb("xTa", [P, R, N])
        h = sb("h", [P, NB, HC])
        e = sb("e", [P, NB, N])
        em = sb("em", [P, NB, N])
        mx = sb("mx", [P, NB])
        neg_mx = sb("neg_mx", [P, NB])
        row_sum = sb("row_sum", [P, NB])
        row_inv = sb("row_inv", [P, NB])
        pr = sb("pr", [P, NB, N])
        prT = sb("prT", [P, NB, N])
        sig = sb("sig", [P, NB, N])
        pick = sb("pick", [P, NB, N])
        rel = sb("rel", [P, R, NB, N])
        xw = sb("xw", [P, NB, R * D])
        res = sb("res", [P, NB, D])
        stats = sb("stats", [P, NB, 6])
        mv = sb("mv", [P, NB, 2])
        var_eps = sb("var_eps", [P, NB])
        rstd = sb("rstd", [P, NB])
        wait_carrier = sb("wait_carrier", [P, 1])

        ps_adjT = bank("ps_adjT", [P, NB, N], BF16)
        ps_xT = bank("ps_xT", [P, 512])
        ps_h = bank("ps_h", [P, 512])
        ps_d = bank("ps_d", [P, 512])
        ps_p = bank("ps_p", [P, NB, N])
        ps_o = bank("ps_o", [P, 4, D])
        ps_xw = bank("ps_xw", [P, NB, R * D])

        weights_in = sem("weights_in")
        zero_set = sem("zero_set")
        ident_set = sem("ident_set")
        ident_bf_set = sem("ident_bf_set")
        a_rep_set = sem("a_rep_set")
        wT_made = sem("wT_made")
        w_ext_set = sem("w_ext_set")
        gen_in = sem("gen_in")
        gen_pe = sem("gen_pe")
        gen_act = sem("gen_act")
        gen_dve = sem("gen_dve")
        gen_pool = sem("gen_pool")
        gen_out = sem("gen_out")

        loads = [
            (w_nat[:, 0, :], W0), (w_nat[:, 1, :], W1),
            (a_col[:, 0, 0:1], a_src0.rearrange("(p a) -> p a", a=1)),
            (a_col[:, 0, 1:2], a_dst0.rearrange("(p a) -> p a", a=1)),
            (a_col[:, 1, 0:1], a1[0:D].rearrange("(p a) -> p a", a=1)),
            (a_col[:, 1, 1:2], a1[D:2 * D].rearrange("(p a) -> p a", a=1)),
            (a2[:, 0:1], a2_0), (a2[:, 1:2], a2_1), (a2[:, 2:3], a2_2), (a2[:, 3:4], a2_3),
            (w3[:, :, :], W3.rearrange("r d o -> d r o")),
        ]
        for k, bb in ((0, bias2), (1, bias3)):
            for b in range(NB):
                loads.append((bias[:, k, b, :], bb.rearrange("(a d) -> a d", a=1).to_broadcast([P, D])))
        WEIGHTS = 16 * len(loads)

        block = ctx.enter_context(nc.Block())

        @block.sync
        def _(sp):
            for dst, src in loads:
                sp.dma_start(dst, src).then_inc(weights_in, 16)

            def load(g):
                sp.dma_start(xg[:, :, :], x_blocks[g]).then_inc(gen_in, 16)
                sp.dma_start(adj_i[:, :, :], adj_blocks[g]).then_inc(gen_in, 16)

            def store(g):
                sp.wait_ge(gen_dve, done(GEN_DVE, g, "norm3"))
                sp.dma_start(out_blocks[g], xg[:, :, :]).then_inc(gen_out, 16)

            load(0)
            with sp.Fori(0, B - 1) as g:
                store(g)
                sp.wait_ge(gen_out, g * 16 + 16)
                load(g + 1)
            store(B - 1)
            sp.wait_ge(gen_out, B * 16)

        @block.gpsimd
        def _(pool):
            nc.gpsimd.memset(zero[:, :], 0.0).then_inc(zero_set, 1)
            nc.gpsimd.memset(minus_half[:, :], -0.5).then_inc(ident_set, 1)
            pool.wait_ge(zero_set, 1)
            nc.gpsimd.affine_select(out=ident[:, :], in_=zero[:, :], compare_op=ALU.not_equal, fill=1.0,
                                    base=0, pattern=[[-1, P]], channel_multiplier=1).then_inc(ident_set, 1)
            pool.wait_ge(ident_set, 2)
            with pool.Fori(0, B) as g:
                for l in range(4):
                    pool.wait_ge(gen_dve, done(GEN_DVE, g, f"var{l}"))
                    nc.gpsimd.tensor_tensor(rstd[:, :], var_eps[:, :], minus_half[:, :], ALU.pow).then_inc(gen_pool, 1)

        @block.scalar
        def _(act):
            with act.Fori(0, B) as g:
                act.wait_ge(gen_pe, done(GEN_PE, g, "adjT"))
                nc.scalar.copy(adjT[:, :, :], ps_adjT[:, :, :]).then_inc(gen_act, 1)
                for l in range(2):
                    act.wait_ge(gen_pe, done(GEN_PE, g, f"xT{l}"))
                    nc.scalar.copy(xT[:, :], ps_xT[:, 0:N]).then_inc(gen_act, 1)
                    act.wait_ge(gen_pe, done(GEN_PE, g, f"h{l}"))
                    nc.scalar.copy(h[:, :, :], ps_h[:, 0:NB * HC].rearrange("p (b c) -> p b c", b=NB)).then_inc(gen_act, 1)
                    act.wait_ge(gen_pe, done(GEN_PE, g, f"dst{l}"))
                    act.wait_ge(gen_act, done(GEN_ACT, g, f"h{l}"))
                    for b in range(NB):
                        last = nc.scalar.activation(e[:, b, :], ps_d[:, 0:N], ACT.Identity, bias=h[:, b, D:D + 1])
                    last.then_inc(gen_act, 1)
                    act.wait_ge(gen_dve, done(GEN_DVE, g, f"negmax{l}"))
                    for b in range(NB):
                        last = nc.scalar.activation(pr[:, b, :], em[:, b, :], ACT.Exp, bias=neg_mx[:, b:b + 1],
                                                    accum_out=row_sum[:, b:b + 1])
                    last.then_inc(gen_act, 1)
                    act.wait_ge(gen_pe, done(GEN_PE, g, f"pT{l}"))
                    nc.scalar.copy(prT[:, :, :], ps_p[:, :, :]).then_inc(gen_act, 1)
                act.wait_ge(gen_pe, done(GEN_PE, g, "xT2"))
                nc.scalar.copy(xT[:, :], ps_xT[:, 0:N]).then_inc(gen_act, 1)
                for r in range(R):
                    act.wait_ge(gen_pe, done(GEN_PE, g, f"score{r}"))
                    nc.scalar.copy(e[:, :, :], ps_p[:, :, :]).then_inc(gen_act, 1)
                    act.wait_ge(gen_dve, done(GEN_DVE, g, f"leaky2{r}"))
                    if r:
                        act.wait_ge(gen_dve, done(GEN_DVE, g, f"pick{r - 1}"))
                    nc.scalar.activation(sig[:, :, :], em[:, :, :], ACT.Sigmoid).then_inc(gen_act, 1)
                act.wait_ge(gen_pe, done(GEN_PE, g, "xT3"))
                nc.scalar.copy(xT[:, :], ps_xT[:, 0:N]).then_inc(gen_act, 1)
                act.wait_ge(gen_pe, done(GEN_PE, g, "xw"))
                for b in range(NB):
                    last = nc.scalar.copy(xw[:, b, :], ps_xw[:, b, :])
                last.then_inc(gen_act, 1)

        @block.vector
        def _(dve):
            dve.wait_ge(ident_set, 2)
            nc.vector.tensor_copy(ident_bf[:, :], ident[:, :]).then_inc(ident_bf_set, 1)
            dve.wait_ge(weights_in, WEIGHTS)
            for l in range(2):
                nc.vector.tensor_scalar(a_rep[:, l, :], zero[:, :], a_col[:, l, 1:2], None, ALU.add).then_inc(a_rep_set, 1)
            for l in range(2):
                dve.wait_ge(wT_made, l + 1)
                nc.vector.tensor_copy(w_ext[:, l, :], ps_h[:, 0:HC])
                nc.vector.tensor_copy(wd_rep[:, l, :], ps_h[:, 256:256 + P]).then_inc(w_ext_set, 1)

            def layernorm(g, l, before):
                dve.wait_ge(gen_dve, done(GEN_DVE, g, before))
                for b in range(NB):
                    last = nc.vector.bn_stats(stats[:, b, :], res[:, b, :])
                last.then_inc(gen_dve, 1)
                dve.wait_ge(gen_dve, done(GEN_DVE, g, f"stats{l}"))
                nc.vector.memset(wait_carrier[:, :], 0.0)
                for b in range(NB):
                    last = nc.vector.bn_aggr(mv[:, b, :], stats[:, b, :])
                last.then_inc(gen_dve, 1)
                dve.wait_ge(gen_dve, done(GEN_DVE, g, f"aggr{l}"))
                nc.vector.tensor_scalar(var_eps[:, :], mv[:, :, 1], EPS, None, ALU.add).then_inc(gen_dve, 1)
                dve.wait_ge(gen_pool, done(GEN_POOL, g, f"pow{l}"))
                for b in range(NB):
                    last = nc.vector.tensor_scalar(xg[:, b, :], res[:, b, :], mv[:, b, 0:1], rstd[:, b:b + 1],
                                                   ALU.subtract, ALU.mult)
                last.then_inc(gen_dve, 1)

            with dve.Fori(0, B) as g:
                dve.wait_ge(gen_in, g * 32 + 32)
                nc.vector.tensor_copy(adj_bf[:, :, :], adj_i[:, :, :]).then_inc(gen_dve, 1)
                dve.wait_ge(gen_dve, done(GEN_DVE, g, "adj"))
                nc.vector.tensor_scalar(edge[:, :, :], adj_bf[:, :, :], 0.0, None, ALU.not_equal).then_inc(gen_dve, 1)
                dve.wait_ge(gen_dve, done(GEN_DVE, g, "edge"))
                for l, neg in ((0, 1e9), (1, 9e15)):
                    nc.vector.tensor_scalar(none[:, l, :, :], edge[:, :, :], -1.0, neg, ALU.add, ALU.mult).then_inc(gen_dve, 1)
                for l in range(2):
                    dve.wait_ge(gen_act, done(GEN_ACT, g, f"sum{l}"))
                    nc.vector.scalar_tensor_tensor(out=em[:, :, :], in0=e[:, :, :], scalar=SLOPE, in1=e[:, :, :],
                                                   op0=ALU.mult, op1=ALU.max).then_inc(gen_dve, 1)
                    dve.wait_ge(gen_dve, done(GEN_DVE, g, f"leaky{l}"))
                    nc.vector.tensor_tensor(em[:, :, :], em[:, :, :], edge[:, :, :], ALU.mult).then_inc(gen_dve, 1)
                    dve.wait_ge(gen_dve, done(GEN_DVE, g, f"keep{l}"))
                    nc.vector.tensor_tensor(em[:, :, :], em[:, :, :], none[:, l, :, :], ALU.add).then_inc(gen_dve, 1)
                    dve.wait_ge(gen_dve, done(GEN_DVE, g, f"mask{l}"))
                    nc.vector.tensor_reduce(mx[:, :], em[:, :, :], AX.X, ALU.max).then_inc(gen_dve, 1)
                    dve.wait_ge(gen_dve, done(GEN_DVE, g, f"max{l}"))
                    nc.vector.tensor_scalar(neg_mx[:, :], mx[:, :], -1.0, None, ALU.mult).then_inc(gen_dve, 1)
                    dve.wait_ge(gen_act, done(GEN_ACT, g, f"exp{l}"))
                    nc.vector.reciprocal(row_inv[:, :], row_sum[:, :]).then_inc(gen_dve, 1)
                    dve.wait_ge(gen_dve, done(GEN_DVE, g, f"rinv{l}"))
                    dve.wait_ge(gen_pe, done(GEN_PE, g, f"out{l}"))
                    for b in range(NB):
                        last = nc.vector.scalar_tensor_tensor(out=res[:, b, :], in0=ps_o[:, b, :], scalar=row_inv[:, b:b + 1],
                                                              in1=xg[:, b, :], op0=ALU.mult, op1=ALU.add)
                    last.then_inc(gen_dve, 1)
                    layernorm(g, l, f"res{l}")
                dve.wait_ge(gen_act, done(GEN_ACT, g, "xT2"))
                for r in range(R):
                    last = nc.vector.tensor_scalar(xTa[:, r, :], xT[:, :], a2[:, r:r + 1], None, ALU.mult)
                last.then_inc(gen_dve, 1)
                for r in range(R):
                    dve.wait_ge(gen_act, done(GEN_ACT, g, f"score{r}"))
                    nc.vector.scalar_tensor_tensor(out=em[:, :, :], in0=e[:, :, :], scalar=SLOPE, in1=e[:, :, :],
                                                   op0=ALU.mult, op1=ALU.max).then_inc(gen_dve, 1)
                    dve.wait_ge(gen_act, done(GEN_ACT, g, f"sigmoid{r}"))
                    if r >= 2:
                        dve.wait_ge(gen_dve, done(GEN_DVE, g, f"sum{r - 1}"))
                    nc.vector.scalar_tensor_tensor(out=(pick if r else prT)[:, :, :], in0=adjT[:, :, :], scalar=float(r + 1),
                                                   in1=sig[:, :, :], op0=ALU.is_equal, op1=ALU.mult).then_inc(gen_dve, 1)
                    if r:
                        dve.wait_ge(gen_dve, done(GEN_DVE, g, f"pick{r}"))
                        nc.vector.tensor_tensor(prT[:, :, :], prT[:, :, :], pick[:, :, :], ALU.add).then_inc(gen_dve, 1)
                for l in (2, 3):
                    if l == 3:
                        for r in range(R):
                            last = nc.vector.tensor_scalar(rel[:, r, :, :], adjT[:, :, :], float(r + 1), None, ALU.is_equal)
                        last.then_inc(gen_dve, 1)
                    dve.wait_ge(gen_pe, done(GEN_PE, g, f"out{l}"))
                    nc.vector.tensor_tensor(res[:, :, :], ps_o[:, 0:NB, :], xg[:, :, :], ALU.add).then_inc(gen_dve, 1)
                    dve.wait_ge(gen_dve, done(GEN_DVE, g, f"add{l}"))
                    nc.vector.tensor_tensor(res[:, :, :], res[:, :, :], bias[:, l - 2, :, :], ALU.add).then_inc(gen_dve, 1)
                    layernorm(g, l, f"res{l}")

        @block.tensor
        def _(pe):
            pe.wait_ge(ident_set, 2)
            pe.wait_ge(ident_bf_set, 1)
            pe.wait_ge(a_rep_set, 2)
            for l in range(2):
                if l:
                    pe.wait_ge(w_ext_set, l)
                nc.tensor.transpose(ps_h[:, 0:D], w_nat[:, l, :], ident[:, :])
                nc.tensor.matmul(ps_h[:, D:D + 2], w_nat[:, l, :], a_col[:, l, :], start=True, stop=True)
                nc.tensor.matmul(ps_h[:, 256:256 + P], w_nat[:, l, :], a_rep[:, l, :], start=True, stop=True).then_inc(wT_made, 1)
            pe.wait_ge(w_ext_set, 2)

            def transpose_x(g, l):
                if l:
                    pe.wait_ge(gen_dve, done(GEN_DVE, g, f"norm{l - 1}"))
                for b in range(NB):
                    last = nc.tensor.transpose(ps_xT[:, b * P:(b + 1) * P], xg[:, b, :], ident[:, :])
                last.then_inc(gen_pe, 1)
                pe.wait_ge(gen_act, done(GEN_ACT, g, f"xT{l}"))

            def aggregate(values):
                for b in range(NB):
                    for c in range(NB):
                        last = nc.tensor.matmul(ps_o[:, b, :], prT[:, c, b * P:(b + 1) * P], values[:, c, 0:D],
                                                start=c == 0, stop=c == NB - 1)
                last.then_inc(gen_pe, 1)

            with pe.Fori(0, B) as g:
                pe.wait_ge(gen_in, g * 32 + 32)
                pe.wait_ge(gen_dve, done(GEN_DVE, g, "adj"))
                for c in range(NB):
                    for b in range(NB):
                        last = nc.tensor.transpose(ps_adjT[:, c, b * P:(b + 1) * P], adj_bf[:, b, c * P:(c + 1) * P], ident_bf[:, :])
                last.then_inc(gen_pe, 1)
                for l in range(2):
                    transpose_x(g, l)
                    for b in range(NB):
                        last = nc.tensor.matmul(ps_h[:, b * HC:(b + 1) * HC], xT[:, b * P:(b + 1) * P], w_ext[:, l, :],
                                                start=True, stop=True)
                    last.then_inc(gen_pe, 1)
                    nc.tensor.matmul(ps_d[:, 0:N], wd_rep[:, l, :], xT[:, :], start=True, stop=True).then_inc(gen_pe, 1)
                    pe.wait_ge(gen_act, done(GEN_ACT, g, f"exp{l}"))
                    for c in range(NB):
                        for b in range(NB):
                            last = nc.tensor.transpose(ps_p[:, c, b * P:(b + 1) * P], pr[:, b, c * P:(c + 1) * P], ident[:, :])
                    last.then_inc(gen_pe, 1)
                    pe.wait_ge(gen_act, done(GEN_ACT, g, f"pT{l}"))
                    aggregate(h)
                transpose_x(g, 2)
                pe.wait_ge(gen_dve, done(GEN_DVE, g, "xTa"))
                for r in range(R):
                    if r:
                        pe.wait_ge(gen_act, done(GEN_ACT, g, f"score{r - 1}"))
                    for c in range(NB):
                        last = nc.tensor.matmul(ps_p[:, c, :], xTa[:, r, c * P:(c + 1) * P], xT[:, :], start=True, stop=True)
                    last.then_inc(gen_pe, 1)
                pe.wait_ge(gen_dve, done(GEN_DVE, g, "sum3"))
                aggregate(xg)
                transpose_x(g, 3)
                for b in range(NB):
                    last = nc.tensor.matmul(ps_xw[:, b, :], xT[:, b * P:(b + 1) * P], w3[:, :, :].rearrange("p r d -> p (r d)"),
                                            start=True, stop=True)
                last.then_inc(gen_pe, 1)
                pe.wait_ge(gen_act, done(GEN_ACT, g, "xw"))
                pe.wait_ge(gen_dve, done(GEN_DVE, g, "rel3"))
                for b in range(NB):
                    for r in range(R):
                        for c in range(NB):
                            last = nc.tensor.matmul(ps_o[:, b, :], rel[:, r, c, b * P:(b + 1) * P], xw[:, c, r * D:(r + 1) * D],
                                                    start=r == 0 and c == 0, stop=r == R - 1 and c == NB - 1)
                last.then_inc(gen_pe, 1)


_INS = ["x", "adj", "L0_gnn_W", "L0_gnn_a_src", "L0_gnn_a_dst", "L1_gnn_W", "L1_gnn_a", "L2_gnn_a0", "L2_gnn_a1",
        "L2_gnn_a2", "L2_gnn_a3", "L2_gnn_bias", "L3_gnn_adj", "L3_gnn_weight", "L3_gnn_bias"]


def kernel(**inputs):
    import numpy as np
    import concourse.bacc as bacc
    from concourse.bass_utils import run_bass_kernel_spmd

    nc = bacc.Bacc("TRN2", target_bir_lowering=False, num_devices=1)
    arrays, args = {}, []
    for name in _INS:
        a = np.ascontiguousarray(inputs[name])
        arrays[f"in_{name}"] = a
        args.append(nc.dram_tensor(f"in_{name}", a.shape, mybir.dt.from_np(a.dtype), kind="ExternalInput").ap())
    shape = np.shape(inputs["x"])
    args.append(nc.dram_tensor("out", shape, F32, kind="ExternalOutput").ap())
    res_gnn_kernel(nc, *args)
    r = run_bass_kernel_spmd(nc, [arrays], core_ids=[0])
    return r.results[0]["out"]
```

```python
from contextlib import ExitStack

import concourse.bass as bass
from concourse import mybir

P = 128
SLOPE = 0.2
EPS = 1e-5
ALU = mybir.AluOpType
ACT = mybir.ActivationFunctionType
AX = mybir.AxisListType
F32 = mybir.dt.float32
BF16 = mybir.dt.bfloat16
F16 = mybir.dt.float16
BIG = 1e30
UP = 4096.0
LOGIT_CAP = 24.0
TINY = 1e-30
I32 = mybir.dt.int32

GEN_PE = ["adjT"]
for _l in "01":
    GEN_PE += [n + _l for n in ("xT", "h", "dst", "pT", "out")]
GEN_PE += ["xT2"] + [f"score{r}" for r in range(4)] + ["out2", "xT3", "xw", "out3"]
GEN_ACT = ["adjT"]
for _l in "01":
    GEN_ACT += [n + _l for n in ("xT", "h", "sum", "exp", "pT")]
GEN_ACT += ["xT2"]
for _r in "0123":
    GEN_ACT += ["score" + _r, "sigmoid" + _r]
GEN_ACT += ["xT3", "xw"]
LN_STEPS = ["res", "stats", "aggr", "var", "norm"]
GEN_DVE = ["adj", "edge", "none0", "none1"]
for _l in "01":
    GEN_DVE += [n + _l for n in ("leaky", "keep", "mask", "max", "negmax", "rinv")] + [n + _l for n in LN_STEPS]
GEN_DVE += ["xTa"]
for _r in "0123":
    GEN_DVE += ["leaky2" + _r, "pick" + _r] + (["sum" + _r] if _r != "0" else [])
GEN_DVE += ["add2"] + [n + "2" for n in LN_STEPS] + ["rel3", "add3"] + [n + "3" for n in LN_STEPS]
GEN_POOL = [f"pow{l}" for l in range(4)]



U = 4
FAST_PE = ["maskT"] + [n + l for l in "01" for n in ("xT", "h", "spread", "out")] + ["xT2", "score", "out2", "agg", "out3"]
FAST_ACT = ["maskT"] + [n + l for l in "01" for n in ("xT", "h", "grow", "factors")] + ["xT2", "sigmoid", "high", "agg"]
FAST_DVE = ["raw", "mask", "off"]
for _l in "01":
    FAST_DVE += [n + _l for n in ("dmax", "shift", "weight", "scale", "rsum", "rinv")] + [n + _l for n in LN_STEPS]
FAST_DVE += ["xTa", "alpha"] + [n + "2" for n in LN_STEPS] + ["low"] + [n + "3" for n in LN_STEPS]
FAST_POOL = ["odd", "odd_sq", "odds", "pow0", "pow1", "bias2", "pow2", "bias3", "pow3"]


def at(steps, t, name, u):
    return t * (len(steps) * U) + steps.index(name) * U + u + 1


def done(steps, g, name):
    return g * len(steps) + steps.index(name) + 1


def res_gnn_kernel(nc, x, adj, W0, a_src0, a_dst0, W1, a1, a2_0, a2_1, a2_2, a2_3, bias2, adj3, W3, bias3, out):
    B, N, D = x.shape
    NB = N // P
    R = W3.shape[0]
    assert D == P and NB == 2 and R == 4
    HC = D + 2

    x_blocks = x.rearrange("g (b p) d -> g p b d", p=P)
    out_blocks = out.rearrange("g (b p) d -> g p b d", p=P)
    adj_blocks = adj.rearrange("g (b p) n -> g p b n", p=P)

    with ExitStack() as ctx:
        def sb(name, shape, dt=F32):
            return ctx.enter_context(nc.sbuf_tensor(name, shape, dt))

        def bank(name, shape, dt=F32):
            return ctx.enter_context(nc.psum_tensor(name, shape, dt))

        def sem(name):
            return ctx.enter_context(nc.semaphore(name))

        zero = sb("zero", [P, P])
        ident = sb("ident", [P, P])
        ident_bf = sb("ident_bf", [P, P], BF16)
        minus_half = sb("minus_half", [P, NB])
        w_nat = sb("w_nat", [P, 2, D])
        a_col = sb("a_col", [P, 2, 2])
        a_rep = sb("a_rep", [P, 2, 2, P])
        w_ext = sb("w_ext", [P, 2, HC])
        wd_rep = sb("wd_rep", [P, 2, P])
        a2 = sb("a2", [P, 4])
        w3 = sb("w3", [P, R, D])
        bias = sb("bias", [P, 2, NB, D])

        xg = sb("xg", [P, NB, D])
        adj_i = sb("adj_i", [P, NB, N], I32)
        adj_bf = sb("adj_bf", [P, NB, N], BF16)
        adjT = sb("adjT", [P, NB, N], BF16)
        edge = sb("edge", [P, NB, N])
        none = sb("none", [P, 2, NB, N])
        xT = sb("xT", [P, N])
        xTa = sb("xTa", [P, R, N])
        h = sb("h", [P, NB, HC])
        e = sb("e", [P, NB, N])
        em = sb("em", [P, NB, N])
        mx = sb("mx", [P, NB])
        neg_mx = sb("neg_mx", [P, NB])
        row_sum = sb("row_sum", [P, NB])
        row_inv = sb("row_inv", [P, NB])
        pr = sb("pr", [P, NB, N])
        prT = sb("prT", [P, NB, N])
        sig = sb("sig", [P, NB, N])
        pick = sb("pick", [P, NB, N])
        rel = sb("rel", [P, R, NB, N])
        xw = sb("xw", [P, NB, R * D])
        res = sb("res", [P, NB, D])
        stats = sb("stats", [P, NB, 6])
        mv = sb("mv", [P, NB, 2])
        var_eps = sb("var_eps", [P, NB])
        rstd = sb("rstd", [P, NB])
        wait_carrier = sb("wait_carrier", [P, 1])

        banks = bank("banks", [P, 8, 512])
        ps_a = [banks[:, 2 * u, :] for u in range(U)]
        ps_b = [banks[:, 2 * u + 1, :] for u in range(U)]
        ps_adjT = banks[:, 0, 0:NB * N // 2].bitcast(BF16).rearrange("p (b n) -> p b n", b=NB)
        ps_xT = banks[:, 1, :]
        ps_h = banks[:, 2, :]
        ps_d = banks[:, 3, :]
        ps_p = banks[:, 4, :].rearrange("p (b n) -> p b n", b=NB)
        ps_o = banks[:, 5, :].rearrange("p (b n) -> p b n", n=D)
        ps_xw = banks[:, 6:8, :]

        def each(name, shape, dt=F32):
            return [sb(f"{name}_{u}", shape, dt) for u in range(U)]

        ws_rep = sb("ws_rep", [P, 2, P])
        big_ident = sb("big_ident", [P, P], BF16)
        x_in = each("x_in", [P, NB, D])
        adj_in = each("adj_in", [P, NB, N], I32)
        raw = each("raw", [P, NB, N], BF16)
        mask = each("mask", [P, NB, N], BF16)
        maskT = each("maskT", [P, NB, N], BF16)
        off = each("off", [P, NB, N], BF16)
        odd = each("odd", [P, NB, N])
        odd_sq = each("odd_sq", [P, NB, N])
        xs = each("xs", [P, NB, D])
        x_out = each("x_out", [P, NB, D])
        xb = each("xb", [P, NB, D])
        fxT = each("fxT", [P, N])
        fxTa = each("fxTa", [P, N])
        fh = each("fh", [P, NB, HC + 2])
        vals = each("vals", [P, NB, D + 1])
        dmax = each("dmax", [P, 2])
        shift = each("shift", [P, 2 * NB])
        fac = each("fac", [P, 2 * NB])
        grow = each("grow", [P, N])
        wgt = each("wgt", [P, NB, N])
        sg = each("sg", [P, 2, NB, N])
        hi = each("hi", [P, NB, D], F16)
        lo = each("lo", [P, NB, D], F16)
        aggT = each("aggT", [P, N])
        frow = each("frow", [P, NB])
        finv = each("finv", [P, NB])
        fres = each("fres", [P, NB, D])
        fstats = each("fstats", [P, NB, 6])
        fmv = each("fmv", [P, NB, 2])
        fvar = each("fvar", [P, NB])
        frstd = each("frstd", [P, NB])
        odd_sum = sb("odd_sum", [P, NB, N])
        logit_max = sb("logit_max", [P, NB, 2])
        logit_min = sb("logit_min", [P, NB, 2])
        row_min = sb("row_min", [P, NB])
        bad = sb("bad", [P, 9])
        ones_col = sb("ones_col", [P, 1])
        redo_f = sb("redo_f", [1, 1])
        redo_i = sb("redo_i", [1, 1], I32)

        weights_in = sem("weights_in")
        fast_adj_in = [sem(f"fast_adj_in_{u}") for u in range(U)]
        fast_x_in = [sem(f"fast_x_in_{u}") for u in range(U)]
        fast_pe = sem("fast_pe")
        fast_act = sem("fast_act")
        fast_dve = sem("fast_dve")
        fast_pool = sem("fast_pool")
        fast_stored = sem("fast_stored")
        met_set = sem("met_set")
        row_min_step = sem("row_min_step")
        bad_step = sem("bad_step")
        bad_summed = sem("bad_summed")
        redo_set = sem("redo_set")
        zero_set = sem("zero_set")
        ident_set = sem("ident_set")
        ident_bf_set = sem("ident_bf_set")
        a_rep_set = sem("a_rep_set")
        wT_made = sem("wT_made")
        w_ext_set = sem("w_ext_set")
        gen_in = sem("gen_in")
        gen_pe = sem("gen_pe")
        gen_act = sem("gen_act")
        gen_dve = sem("gen_dve")
        gen_pool = sem("gen_pool")
        gen_out = sem("gen_out")

        loads = [
            (w_nat[:, 0, :], W0), (w_nat[:, 1, :], W1),
            (a_col[:, 0, 0:1], a_src0.rearrange("(p a) -> p a", a=1)),
            (a_col[:, 0, 1:2], a_dst0.rearrange("(p a) -> p a", a=1)),
            (a_col[:, 1, 0:1], a1[0:D].rearrange("(p a) -> p a", a=1)),
            (a_col[:, 1, 1:2], a1[D:2 * D].rearrange("(p a) -> p a", a=1)),
            (a2[:, 0:1], a2_0), (a2[:, 1:2], a2_1), (a2[:, 2:3], a2_2), (a2[:, 3:4], a2_3),
            (w3[:, :, :], W3.rearrange("r d o -> d r o")),
        ]
        for k, bb in ((0, bias2), (1, bias3)):
            for b in range(NB):
                loads.append((bias[:, k, b, :], bb.rearrange("(a d) -> a d", a=1).to_broadcast([P, D])))
        WEIGHTS = 16 * (len(loads) - U)
        T = B // U

        block = ctx.enter_context(nc.Block())

        @block.sync
        def _(sp):
            for n, (dst, src) in enumerate(loads):
                sp.dma_start(dst, src).then_inc(weights_in if n < len(loads) - U else fast_stored, 16)

            def fast_load_adj(t, u):
                sp.dma_start(adj_in[u][:, :, :], adj_blocks[t * U + u]).then_inc(fast_adj_in[u], 16)

            def fast_load_x(t, u):
                sp.dma_start(x_in[u][:, :, :], x_blocks[t * U + u]).then_inc(fast_x_in[u], 16)

            def fast_store(t, u):
                sp.wait_ge(fast_dve, at(FAST_DVE, t, "norm3", u))
                sp.dma_start(out_blocks[t * U + u], x_out[u][:, :, :]).then_inc(fast_stored, 16)

            for u in range(U):
                fast_load_adj(0, u)
                fast_load_x(0, u)
            with sp.Fori(0, T - 1) as t:
                for u in range(U):
                    sp.wait_ge(fast_dve, at(FAST_DVE, t, "mask", u))
                    fast_load_adj(t + 1, u)
                for u in range(U):
                    sp.wait_ge(fast_dve, at(FAST_DVE, t, "res0", u))
                    fast_load_x(t + 1, u)
                for u in range(U):
                    fast_store(t, u)
            for u in range(U):
                fast_store(T - 1, u)
            sp.wait_ge(fast_stored, 16 * U * (T + 1))

            sp.wait_ge(redo_set, 1)
            with sp.If(sp.value_load(redo_i[0:1, 0:1], min_val=0, max_val=1)):
                def load(g):
                    sp.dma_start(xg[:, :, :], x_blocks[g]).then_inc(gen_in, 16)
                    sp.dma_start(adj_i[:, :, :], adj_blocks[g]).then_inc(gen_in, 16)

                def store(g):
                    sp.wait_ge(gen_dve, done(GEN_DVE, g, "norm3"))
                    sp.dma_start(out_blocks[g], xg[:, :, :]).then_inc(gen_out, 16)

                load(0)
                with sp.Fori(0, B - 1) as g:
                    store(g)
                    sp.wait_ge(gen_out, g * 16 + 16)
                    load(g + 1)
                store(B - 1)
                sp.wait_ge(gen_out, B * 16)

        @block.gpsimd
        def _(pool):
            nc.gpsimd.memset(zero[:, :], 0.0).then_inc(zero_set, 1)
            nc.gpsimd.memset(minus_half[:, :], -0.5).then_inc(ident_set, 1)
            pool.wait_ge(zero_set, 1)
            nc.gpsimd.affine_select(out=ident[:, :], in_=zero[:, :], compare_op=ALU.not_equal, fill=1.0,
                                    base=0, pattern=[[-1, P]], channel_multiplier=1).then_inc(ident_set, 1)
            nc.gpsimd.memset(odd_sum[:, :, :], 0.0).then_inc(ident_set, 1)
            pool.wait_ge(ident_set, 3)
            with pool.Fori(0, T) as t:
                for u in range(U):
                    pool.wait_ge(fast_dve, at(FAST_DVE, t, "mask", u))
                    nc.gpsimd.tensor_tensor(odd[u][:, :, :], raw[u][:, :, :], mask[u][:, :, :], ALU.subtract).then_inc(fast_pool, 1)
                for u in range(U):
                    pool.wait_ge(fast_pool, at(FAST_POOL, t, "odd", u))
                    nc.gpsimd.tensor_tensor(odd_sq[u][:, :, :], odd[u][:, :, :], odd[u][:, :, :], ALU.mult).then_inc(fast_pool, 1)
                for u in range(U):
                    pool.wait_ge(fast_pool, at(FAST_POOL, t, "odds", u) - (1 if u else U))
                    nc.gpsimd.tensor_tensor(odd_sum[:, :, :], odd_sum[:, :, :], odd_sq[u][:, :, :], ALU.add).then_inc(fast_pool, 1)
                for l in range(4):
                    if l >= 2:
                        for u in range(U):
                            pool.wait_ge(fast_dve, at(FAST_DVE, t, f"norm{l - 1}", u))
                            nc.gpsimd.tensor_tensor(xb[u][:, :, :], xs[u][:, :, :], bias[:, l - 2, :, :], ALU.add).then_inc(fast_pool, 1)
                    for u in range(U):
                        pool.wait_ge(fast_dve, at(FAST_DVE, t, f"var{l}", u))
                        nc.gpsimd.tensor_tensor(frstd[u][:, :], fvar[u][:, :], minus_half[:, :], ALU.pow).then_inc(fast_pool, 1)
            pool.wait_ge(redo_set, 1)
            with pool.If(pool.value_load(redo_i[0:1, 0:1], min_val=0, max_val=1)):
                with pool.Fori(0, B) as g:
                    for l in range(4):
                        pool.wait_ge(gen_dve, done(GEN_DVE, g, f"var{l}"))
                        nc.gpsimd.tensor_tensor(rstd[:, :], var_eps[:, :], minus_half[:, :], ALU.pow).then_inc(gen_pool, 1)

        @block.scalar
        def _(act):
            act.wait_ge(met_set, 3 + U)
            with act.Fori(0, T) as t:
                for u in range(U):
                    act.wait_ge(fast_pe, at(FAST_PE, t, "maskT", u))
                    nc.scalar.copy(maskT[u][:, :, :], ps_b[u][:, 0:N].bitcast(BF16).rearrange("p (b n) -> p b n", b=NB)).then_inc(fast_act, 1)

                def copy_xT(l):
                    for u in range(U):
                        act.wait_ge(fast_pe, at(FAST_PE, t, f"xT{l}", u))
                        nc.scalar.copy(fxT[u][:, :], ps_a[u][:, 0:N]).then_inc(fast_act, 1)

                for l in range(2):
                    copy_xT(l)
                    for u in range(U):
                        act.wait_ge(fast_pe, at(FAST_PE, t, f"h{l}", u))
                        nc.scalar.copy(fh[u][:, :, 1:1 + HC], ps_b[u][:, 0:NB * HC].rearrange("p (b c) -> p b c", b=NB)).then_inc(fast_act, 1)
                    for u in range(U):
                        act.wait_ge(fast_pe, at(FAST_PE, t, f"spread{l}", u))
                        act.wait_ge(fast_dve, at(FAST_DVE, t, f"shift{l}", u))
                        nc.scalar.activation(grow[u][:, :], ps_a[u][:, 0:N], ACT.Exp, bias=dmax[u][:, 1:2], scale=1 - SLOPE).then_inc(fast_act, 1)
                    for u in range(U):
                        nc.scalar.activation(fac[u][:, :], shift[u][:, :], ACT.Exp).then_inc(fast_act, 1)
                copy_xT(2)
                for u in range(U):
                    act.wait_ge(fast_pe, at(FAST_PE, t, "score", u))
                    for k, slope in enumerate((1.0, SLOPE)):
                        last = nc.scalar.activation(sg[u][:, k, :, :], ps_a[u].rearrange("p (b n) -> p b n", b=NB), ACT.Sigmoid, scale=slope)
                    last.then_inc(fast_act, 1)
                for u in range(U):
                    act.wait_ge(fast_dve, at(FAST_DVE, t, "norm2", u))
                    nc.scalar.activation(hi[u][:, :, :], xs[u][:, :, :], ACT.Copy, scale=UP).then_inc(fast_act, 1)
                for u in range(U):
                    act.wait_ge(fast_pe, at(FAST_PE, t, "agg", u))
                    nc.scalar.activation(aggT[u][:, :], ps_a[u][:, 0:N], ACT.Copy, scale=1 / UP).then_inc(fast_act, 1)

            act.wait_ge(redo_set, 1)
            with act.If(act.value_load(redo_i[0:1, 0:1], min_val=0, max_val=1)):
                with act.Fori(0, B) as g:
                    act.wait_ge(gen_pe, done(GEN_PE, g, "adjT"))
                    nc.scalar.copy(adjT[:, :, :], ps_adjT[:, :, :]).then_inc(gen_act, 1)
                    for l in range(2):
                        act.wait_ge(gen_pe, done(GEN_PE, g, f"xT{l}"))
                        nc.scalar.copy(xT[:, :], ps_xT[:, 0:N]).then_inc(gen_act, 1)
                        act.wait_ge(gen_pe, done(GEN_PE, g, f"h{l}"))
                        nc.scalar.copy(h[:, :, :], ps_h[:, 0:NB * HC].rearrange("p (b c) -> p b c", b=NB)).then_inc(gen_act, 1)
                        act.wait_ge(gen_pe, done(GEN_PE, g, f"dst{l}"))
                        act.wait_ge(gen_act, done(GEN_ACT, g, f"h{l}"))
                        for b in range(NB):
                            last = nc.scalar.activation(e[:, b, :], ps_d[:, 0:N], ACT.Identity, bias=h[:, b, D:D + 1])
                        last.then_inc(gen_act, 1)
                        act.wait_ge(gen_dve, done(GEN_DVE, g, f"negmax{l}"))
                        for b in range(NB):
                            last = nc.scalar.activation(pr[:, b, :], em[:, b, :], ACT.Exp, bias=neg_mx[:, b:b + 1],
                                                        accum_out=row_sum[:, b:b + 1])
                        last.then_inc(gen_act, 1)
                        act.wait_ge(gen_pe, done(GEN_PE, g, f"pT{l}"))
                        nc.scalar.copy(prT[:, :, :], ps_p[:, :, :]).then_inc(gen_act, 1)
                    act.wait_ge(gen_pe, done(GEN_PE, g, "xT2"))
                    nc.scalar.copy(xT[:, :], ps_xT[:, 0:N]).then_inc(gen_act, 1)
                    for r in range(R):
                        act.wait_ge(gen_pe, done(GEN_PE, g, f"score{r}"))
                        nc.scalar.copy(e[:, :, :], ps_p[:, :, :]).then_inc(gen_act, 1)
                        act.wait_ge(gen_dve, done(GEN_DVE, g, f"leaky2{r}"))
                        if r:
                            act.wait_ge(gen_dve, done(GEN_DVE, g, f"pick{r - 1}"))
                        nc.scalar.activation(sig[:, :, :], em[:, :, :], ACT.Sigmoid).then_inc(gen_act, 1)
                    act.wait_ge(gen_pe, done(GEN_PE, g, "xT3"))
                    nc.scalar.copy(xT[:, :], ps_xT[:, 0:N]).then_inc(gen_act, 1)
                    act.wait_ge(gen_pe, done(GEN_PE, g, "xw"))
                    for b in range(NB):
                        last = nc.scalar.copy(xw[:, b, :], ps_xw[:, b, :])
                    last.then_inc(gen_act, 1)

        @block.vector
        def _(dve):
            dve.wait_ge(ident_set, 2)
            nc.vector.tensor_copy(ident_bf[:, :], ident[:, :]).then_inc(ident_bf_set, 1)
            nc.vector.tensor_scalar(big_ident[:, :], ident[:, :], BIG, None, ALU.mult).then_inc(ident_bf_set, 1)
            nc.vector.memset(ones_col[:, :], 1.0).then_inc(ident_bf_set, 1)
            nc.vector.memset(logit_max[:, :, :], 0.0).then_inc(met_set, 1)
            nc.vector.memset(logit_min[:, :, :], 0.0).then_inc(met_set, 1)
            nc.vector.memset(row_min[:, :], 1.0).then_inc(met_set, 1)
            for u in range(U):
                nc.vector.memset(fh[u][:, :, 0:1], 1.0).then_inc(met_set, 1)
            dve.wait_ge(met_set, 3 + U)
            dve.wait_ge(weights_in, WEIGHTS)
            for l in range(2):
                for k in range(2):
                    nc.vector.tensor_scalar(a_rep[:, l, k, :], zero[:, :], a_col[:, l, k:k + 1], None, ALU.add).then_inc(a_rep_set, 1)
            for l in range(2):
                dve.wait_ge(wT_made, l + 1)
                nc.vector.tensor_copy(w_ext[:, l, :], ps_h[:, 0:HC])
                nc.vector.tensor_copy(ws_rep[:, l, :], ps_h[:, 256:256 + P])
                nc.vector.tensor_copy(wd_rep[:, l, :], ps_h[:, 384:384 + P]).then_inc(w_ext_set, 1)

            def fast_layernorm(t, l):
                dst = x_out if l == 3 else xs
                for u in range(U):
                    dve.wait_ge(fast_dve, at(FAST_DVE, t, f"res{l}", u))
                    for b in range(NB):
                        last = nc.vector.bn_stats(fstats[u][:, b, :], fres[u][:, b, :])
                    last.then_inc(fast_dve, 1)
                dve.wait_ge(fast_dve, at(FAST_DVE, t, f"stats{l}", U - 1))
                nc.vector.memset(wait_carrier[:, :], 0.0)
                for u in range(U):
                    for b in range(NB):
                        last = nc.vector.bn_aggr(fmv[u][:, b, :], fstats[u][:, b, :])
                    last.then_inc(fast_dve, 1)
                for u in range(U):
                    dve.wait_ge(fast_dve, at(FAST_DVE, t, f"aggr{l}", u))
                    nc.vector.tensor_scalar(fvar[u][:, :], fmv[u][:, :, 1], EPS, None, ALU.add).then_inc(fast_dve, 1)
                for u in range(U):
                    dve.wait_ge(fast_pool, at(FAST_POOL, t, f"pow{l}", u))
                    if l == 3:
                        dve.wait_ge(fast_stored, t * (16 * U) + 16 * U)
                    for b in range(NB):
                        last = nc.vector.tensor_scalar(dst[u][:, b, :], fres[u][:, b, :], fmv[u][:, b, 0:1], frstd[u][:, b:b + 1],
                                                       ALU.subtract, ALU.mult)
                    last.then_inc(fast_dve, 1)

            with dve.Fori(0, T) as t:
                for u in range(U):
                    dve.wait_ge(fast_adj_in[u], t * 16 + 16)
                    nc.vector.tensor_copy(raw[u][:, :, :], adj_in[u][:, :, :]).then_inc(fast_dve, 1)
                for u in range(U):
                    dve.wait_ge(fast_dve, at(FAST_DVE, t, "raw", u))
                    nc.vector.tensor_scalar(mask[u][:, :, :], raw[u][:, :, :], 0.0, None, ALU.not_equal).then_inc(fast_dve, 1)
                for u in range(U):
                    dve.wait_ge(fast_act, at(FAST_ACT, t, "maskT", u))
                    nc.vector.tensor_scalar(off[u][:, :, :], maskT[u][:, :, :], -1.0, None, ALU.add).then_inc(fast_dve, 1)
                for l in range(2):
                    x_l = x_in if l == 0 else xs
                    for u in range(U):
                        dve.wait_ge(fast_pe, at(FAST_PE, t, f"spread{l}", u))
                        nc.vector.tensor_reduce(dmax[u][:, 0:1], ps_a[u][:, N:2 * N], AX.X, ALU.max).then_inc(fast_dve, 1)
                    for u in range(U):
                        dve.wait_ge(fast_act, at(FAST_ACT, t, f"h{l}", u))
                        dve.wait_ge(fast_dve, at(FAST_DVE, t, f"dmax{l}", u))
                        nc.vector.tensor_scalar(dmax[u][:, 1:2], dmax[u][:, 0:1], 1 - SLOPE, None, ALU.mult)
                        nc.vector.tensor_scalar(shift[u][:, 0:NB], fh[u][:, :, D + 2], dmax[u][:, 0:1], None, ALU.subtract)
                        nc.vector.tensor_scalar(shift[u][:, NB:2 * NB], fh[u][:, :, D + 2], dmax[u][:, 0:1], SLOPE - 1,
                                                ALU.subtract, ALU.mult)
                        nc.vector.tensor_tensor(logit_max[:, :, :], logit_max[:, :, :], fh[u][:, :, D + 1:D + 3], ALU.max)
                        nc.vector.tensor_tensor(logit_min[:, :, :], logit_min[:, :, :], fh[u][:, :, D + 1:D + 3],
                                                ALU.min).then_inc(fast_dve, 1)
                        dve.wait_ge(fast_dve, at(FAST_DVE, t, f"shift{l}", u))
                    for u in range(U):
                        dve.wait_ge(fast_act, at(FAST_ACT, t, f"factors{l}", u))
                        for c in range(NB):
                            last = nc.vector.scalar_tensor_tensor(out=wgt[u][:, c, :], in0=grow[u][:, :], scalar=fac[u][:, NB + c:NB + c + 1],
                                                                  in1=maskT[u][:, c, :], op0=ALU.max, op1=ALU.mult)
                        last.then_inc(fast_dve, 1)
                    for u in range(U):
                        for c in range(NB):
                            last = nc.vector.tensor_scalar(vals[u][:, c, :], fh[u][:, c, 0:D + 1], fac[u][:, c:c + 1], None, ALU.mult)
                        last.then_inc(fast_dve, 1)
                    for u in range(U):
                        sums = ps_b[u][:, 0:NB * (D + 1)].rearrange("p (b c) -> p b c", b=NB)
                        dve.wait_ge(fast_pe, at(FAST_PE, t, f"out{l}", u))
                        nc.vector.tensor_scalar(frow[u][:, :], sums[:, :, 0], TINY, None, ALU.max).then_inc(fast_dve, 1)
                    for u in range(U):
                        dve.wait_ge(fast_dve, at(FAST_DVE, t, f"rsum{l}", u))
                        nc.vector.reciprocal(finv[u][:, :], frow[u][:, :]).then_inc(fast_dve, 1)
                    for u in range(U):
                        nc.vector.tensor_tensor(row_min[:, :], row_min[:, :], frow[u][:, :], ALU.min).then_inc(row_min_step, 1)
                        dve.wait_ge(row_min_step, t * (2 * U) + l * U + u + 1)
                    dve.wait_ge(fast_dve, at(FAST_DVE, t, f"rinv{l}", U - 1))
                    for u in range(U):
                        sums = ps_b[u][:, 0:NB * (D + 1)].rearrange("p (b c) -> p b c", b=NB)
                        for b in range(NB):
                            last = nc.vector.scalar_tensor_tensor(out=fres[u][:, b, :], in0=sums[:, b, 1:D + 1], scalar=finv[u][:, b:b + 1],
                                                                  in1=x_l[u][:, b, :], op0=ALU.mult, op1=ALU.add)
                        last.then_inc(fast_dve, 1)
                    fast_layernorm(t, l)
                for u in range(U):
                    dve.wait_ge(fast_act, at(FAST_ACT, t, "xT2", u))
                    nc.vector.tensor_scalar(fxTa[u][:, :], fxT[u][:, :], a2[:, 0:1], None, ALU.mult).then_inc(fast_dve, 1)
                for u in range(U):
                    dve.wait_ge(fast_act, at(FAST_ACT, t, "sigmoid", u))
                    nc.vector.tensor_tensor(wgt[u][:, :, :], sg[u][:, 0, :, :], sg[u][:, 1, :, :], ALU.max).then_inc(fast_dve, 1)
                for l in range(2, 4):
                    if l == 3:
                        for u in range(U):
                            dve.wait_ge(fast_act, at(FAST_ACT, t, "high", u))
                            nc.vector.scalar_tensor_tensor(out=lo[u][:, :, :], in0=xs[u][:, :, :], scalar=UP, in1=hi[u][:, :, :],
                                                           op0=ALU.mult, op1=ALU.subtract).then_inc(fast_dve, 1)
                    for u in range(U):
                        dve.wait_ge(fast_pool, at(FAST_POOL, t, f"bias{l}", u))
                        dve.wait_ge(fast_pe, at(FAST_PE, t, f"out{l}", u))
                        nc.vector.tensor_tensor(fres[u][:, :, :], ps_b[u][:, 0:NB * D].rearrange("p (b c) -> p b c", b=NB), xb[u][:, :, :],
                                                ALU.add).then_inc(fast_dve, 1)
                    fast_layernorm(t, l)

            dve.wait_ge(fast_pool, T * len(FAST_POOL) * U)
            dve.wait_ge(fast_dve, T * len(FAST_DVE) * U)
            nc.vector.tensor_reduce(bad[:, 0:1], odd_sum[:, :, :], AX.XY, ALU.max)
            nc.vector.tensor_reduce(bad[:, 1:2], logit_max[:, :, :], AX.XY, ALU.max)
            nc.vector.tensor_reduce(bad[:, 7:8], logit_min[:, :, :], AX.XY, ALU.min)
            nc.vector.tensor_reduce(bad[:, 2:3], row_min[:, :], AX.X, ALU.min).then_inc(bad_step, 1)
            dve.wait_ge(bad_step, 1)
            nc.vector.tensor_scalar(bad[:, 3:4], bad[:, 0:1], 0.0, None, ALU.is_gt)
            nc.vector.tensor_scalar(bad[:, 4:5], bad[:, 1:2], LOGIT_CAP, None, ALU.is_gt)
            nc.vector.tensor_scalar(bad[:, 6:7], bad[:, 7:8], -LOGIT_CAP, None, ALU.is_lt)
            nc.vector.tensor_scalar(bad[:, 5:6], bad[:, 2:3], TINY, None, ALU.is_le).then_inc(bad_step, 1)
            dve.wait_ge(bad_step, 2)
            nc.vector.tensor_reduce(bad[:, 8:9], bad[:, 3:7], AX.X, ALU.max).then_inc(bad_step, 1)
            dve.wait_ge(bad_summed, 1)
            nc.vector.tensor_scalar(redo_i[:, :], ps_a[0][0:1, 0:1], 0.0, None, ALU.is_gt).then_inc(redo_set, 1)

            def layernorm(g, l, before):
                dve.wait_ge(gen_dve, done(GEN_DVE, g, before))
                for b in range(NB):
                    last = nc.vector.bn_stats(stats[:, b, :], res[:, b, :])
                last.then_inc(gen_dve, 1)
                dve.wait_ge(gen_dve, done(GEN_DVE, g, f"stats{l}"))
                nc.vector.memset(wait_carrier[:, :], 0.0)
                for b in range(NB):
                    last = nc.vector.bn_aggr(mv[:, b, :], stats[:, b, :])
                last.then_inc(gen_dve, 1)
                dve.wait_ge(gen_dve, done(GEN_DVE, g, f"aggr{l}"))
                nc.vector.tensor_scalar(var_eps[:, :], mv[:, :, 1], EPS, None, ALU.add).then_inc(gen_dve, 1)
                dve.wait_ge(gen_pool, done(GEN_POOL, g, f"pow{l}"))
                for b in range(NB):
                    last = nc.vector.tensor_scalar(xg[:, b, :], res[:, b, :], mv[:, b, 0:1], rstd[:, b:b + 1],
                                                   ALU.subtract, ALU.mult)
                last.then_inc(gen_dve, 1)

            dve.wait_ge(redo_set, 1)
            with dve.If(dve.value_load(redo_i[0:1, 0:1], min_val=0, max_val=1)):
                with dve.Fori(0, B) as g:
                    dve.wait_ge(gen_in, g * 32 + 32)
                    nc.vector.tensor_copy(adj_bf[:, :, :], adj_i[:, :, :]).then_inc(gen_dve, 1)
                    dve.wait_ge(gen_dve, done(GEN_DVE, g, "adj"))
                    nc.vector.tensor_scalar(edge[:, :, :], adj_bf[:, :, :], 0.0, None, ALU.not_equal).then_inc(gen_dve, 1)
                    dve.wait_ge(gen_dve, done(GEN_DVE, g, "edge"))
                    for l, neg in ((0, 1e9), (1, 9e15)):
                        nc.vector.tensor_scalar(none[:, l, :, :], edge[:, :, :], -1.0, neg, ALU.add, ALU.mult).then_inc(gen_dve, 1)
                    for l in range(2):
                        dve.wait_ge(gen_act, done(GEN_ACT, g, f"sum{l}"))
                        nc.vector.scalar_tensor_tensor(out=em[:, :, :], in0=e[:, :, :], scalar=SLOPE, in1=e[:, :, :],
                                                       op0=ALU.mult, op1=ALU.max).then_inc(gen_dve, 1)
                        dve.wait_ge(gen_dve, done(GEN_DVE, g, f"leaky{l}"))
                        nc.vector.tensor_tensor(em[:, :, :], em[:, :, :], edge[:, :, :], ALU.mult).then_inc(gen_dve, 1)
                        dve.wait_ge(gen_dve, done(GEN_DVE, g, f"keep{l}"))
                        nc.vector.tensor_tensor(em[:, :, :], em[:, :, :], none[:, l, :, :], ALU.add).then_inc(gen_dve, 1)
                        dve.wait_ge(gen_dve, done(GEN_DVE, g, f"mask{l}"))
                        nc.vector.tensor_reduce(mx[:, :], em[:, :, :], AX.X, ALU.max).then_inc(gen_dve, 1)
                        dve.wait_ge(gen_dve, done(GEN_DVE, g, f"max{l}"))
                        nc.vector.tensor_scalar(neg_mx[:, :], mx[:, :], -1.0, None, ALU.mult).then_inc(gen_dve, 1)
                        dve.wait_ge(gen_act, done(GEN_ACT, g, f"exp{l}"))
                        nc.vector.reciprocal(row_inv[:, :], row_sum[:, :]).then_inc(gen_dve, 1)
                        dve.wait_ge(gen_dve, done(GEN_DVE, g, f"rinv{l}"))
                        dve.wait_ge(gen_pe, done(GEN_PE, g, f"out{l}"))
                        for b in range(NB):
                            last = nc.vector.scalar_tensor_tensor(out=res[:, b, :], in0=ps_o[:, b, :], scalar=row_inv[:, b:b + 1],
                                                                  in1=xg[:, b, :], op0=ALU.mult, op1=ALU.add)
                        last.then_inc(gen_dve, 1)
                        layernorm(g, l, f"res{l}")
                    dve.wait_ge(gen_act, done(GEN_ACT, g, "xT2"))
                    for r in range(R):
                        last = nc.vector.tensor_scalar(xTa[:, r, :], xT[:, :], a2[:, r:r + 1], None, ALU.mult)
                    last.then_inc(gen_dve, 1)
                    for r in range(R):
                        dve.wait_ge(gen_act, done(GEN_ACT, g, f"score{r}"))
                        nc.vector.scalar_tensor_tensor(out=em[:, :, :], in0=e[:, :, :], scalar=SLOPE, in1=e[:, :, :],
                                                       op0=ALU.mult, op1=ALU.max).then_inc(gen_dve, 1)
                        dve.wait_ge(gen_act, done(GEN_ACT, g, f"sigmoid{r}"))
                        if r >= 2:
                            dve.wait_ge(gen_dve, done(GEN_DVE, g, f"sum{r - 1}"))
                        nc.vector.scalar_tensor_tensor(out=(pick if r else prT)[:, :, :], in0=adjT[:, :, :], scalar=float(r + 1),
                                                       in1=sig[:, :, :], op0=ALU.is_equal, op1=ALU.mult).then_inc(gen_dve, 1)
                        if r:
                            dve.wait_ge(gen_dve, done(GEN_DVE, g, f"pick{r}"))
                            nc.vector.tensor_tensor(prT[:, :, :], prT[:, :, :], pick[:, :, :], ALU.add).then_inc(gen_dve, 1)
                    for l in (2, 3):
                        if l == 3:
                            for r in range(R):
                                last = nc.vector.tensor_scalar(rel[:, r, :, :], adjT[:, :, :], float(r + 1), None, ALU.is_equal)
                            last.then_inc(gen_dve, 1)
                        dve.wait_ge(gen_pe, done(GEN_PE, g, f"out{l}"))
                        nc.vector.tensor_tensor(res[:, :, :], ps_o[:, 0:NB, :], xg[:, :, :], ALU.add).then_inc(gen_dve, 1)
                        dve.wait_ge(gen_dve, done(GEN_DVE, g, f"add{l}"))
                        nc.vector.tensor_tensor(res[:, :, :], res[:, :, :], bias[:, l - 2, :, :], ALU.add).then_inc(gen_dve, 1)
                        layernorm(g, l, f"res{l}")

        @block.tensor
        def _(pe):
            pe.wait_ge(ident_set, 2)
            pe.wait_ge(ident_bf_set, 3)
            pe.wait_ge(a_rep_set, 4)
            for l in range(2):
                if l:
                    pe.wait_ge(w_ext_set, l)
                nc.tensor.transpose(ps_h[:, 0:D], w_nat[:, l, :], ident[:, :])
                nc.tensor.matmul(ps_h[:, D:D + 2], w_nat[:, l, :], a_col[:, l, :], start=True, stop=True)
                nc.tensor.matmul(ps_h[:, 256:384], w_nat[:, l, :], a_rep[:, l, 0, :], start=True, stop=True)
                nc.tensor.matmul(ps_h[:, 384:512], w_nat[:, l, :], a_rep[:, l, 1, :], start=True, stop=True).then_inc(wT_made, 1)
            pe.wait_ge(w_ext_set, 2)

            def fast_xT(t, l):
                for u in range(U):
                    x_l = x_in if l == 0 else xs
                    if l:
                        pe.wait_ge(fast_dve, at(FAST_DVE, t, f"norm{l - 1}", u))
                    else:
                        pe.wait_ge(fast_x_in[u], t * 16 + 16)
                    for b in range(NB):
                        last = nc.tensor.transpose(ps_a[u][:, b * P:(b + 1) * P], x_l[u][:, b, :], ident[:, :])
                    last.then_inc(fast_pe, 1)

            with pe.Fori(0, T) as t:
                for u in range(U):
                    view = ps_b[u][:, 0:N].bitcast(BF16).rearrange("p (b n) -> p b n", b=NB)
                    pe.wait_ge(fast_dve, at(FAST_DVE, t, "mask", u))
                    for c in range(NB):
                        for b in range(NB):
                            last = nc.tensor.transpose(view[:, c, b * P:(b + 1) * P], mask[u][:, b, c * P:(c + 1) * P], ident_bf[:, :])
                    last.then_inc(fast_pe, 1)
                for l in range(2):
                    fast_xT(t, l)
                    for u in range(U):
                        pe.wait_ge(fast_act, at(FAST_ACT, t, f"xT{l}", u))
                        for b in range(NB):
                            last = nc.tensor.matmul(ps_b[u][:, b * HC:(b + 1) * HC], fxT[u][:, b * P:(b + 1) * P], w_ext[:, l, :],
                                                    start=True, stop=True)
                        last.then_inc(fast_pe, 1)
                    for u in range(U):
                        nc.tensor.matmul(ps_a[u][:, 0:N], ws_rep[:, l, :], fxT[u][:, :], start=True, stop=True)
                        nc.tensor.matmul(ps_a[u][:, N:2 * N], wd_rep[:, l, :], fxT[u][:, :], start=True, stop=True).then_inc(fast_pe, 1)
                    for u in range(U):
                        pe.wait_ge(fast_dve, at(FAST_DVE, t, f"scale{l}", u))
                        for b in range(NB):
                            for c in range(NB):
                                last = nc.tensor.matmul(ps_b[u][:, b * (D + 1):(b + 1) * (D + 1)], wgt[u][:, c, b * P:(b + 1) * P],
                                                        vals[u][:, c, :], start=c == 0, stop=c == NB - 1)
                        last.then_inc(fast_pe, 1)
                fast_xT(t, 2)
                for u in range(U):
                    pe.wait_ge(fast_dve, at(FAST_DVE, t, "xTa", u))
                    for c in range(NB):
                        nc.tensor.matmul(ps_a[u][:, c * N:(c + 1) * N], fxTa[u][:, c * P:(c + 1) * P], fxT[u][:, :], start=True, stop=False)
                        last = nc.tensor.matmul(ps_a[u][:, c * N:(c + 1) * N], big_ident[:, :], off[u][:, c, :], start=False, stop=True)
                    last.then_inc(fast_pe, 1)
                for u in range(U):
                    pe.wait_ge(fast_dve, at(FAST_DVE, t, "alpha", u))
                    for b in range(NB):
                        for c in range(NB):
                            last = nc.tensor.matmul(ps_b[u][:, b * D:(b + 1) * D], wgt[u][:, c, b * P:(b + 1) * P], xs[u][:, c, :],
                                                    start=c == 0, stop=c == NB - 1)
                    last.then_inc(fast_pe, 1)
                for u in range(U):
                    pe.wait_ge(fast_dve, at(FAST_DVE, t, "low", u))
                    for c in range(NB):
                        for part in (hi, lo):
                            last = nc.tensor.matmul(ps_a[u][:, 0:N], part[u][:, c, :], maskT[u][:, c, :],
                                                    start=c == 0 and part is hi, stop=c == NB - 1 and part is lo)
                    last.then_inc(fast_pe, 1)
                for u in range(U):
                    pe.wait_ge(fast_act, at(FAST_ACT, t, "agg", u))
                    for b in range(NB):
                        last = nc.tensor.matmul(ps_b[u][:, b * D:(b + 1) * D], aggT[u][:, b * P:(b + 1) * P], w3[:, 0, :], start=True, stop=True)
                    last.then_inc(fast_pe, 1)

            pe.wait_ge(bad_step, 3)
            nc.tensor.matmul(ps_a[0][0:1, 0:1], bad[:, 8:9], ones_col[:, :], start=True, stop=True).then_inc(bad_summed, 1)

            def transpose_x(g, l):
                if l:
                    pe.wait_ge(gen_dve, done(GEN_DVE, g, f"norm{l - 1}"))
                for b in range(NB):
                    last = nc.tensor.transpose(ps_xT[:, b * P:(b + 1) * P], xg[:, b, :], ident[:, :])
                last.then_inc(gen_pe, 1)
                pe.wait_ge(gen_act, done(GEN_ACT, g, f"xT{l}"))

            def aggregate(values):
                for b in range(NB):
                    for c in range(NB):
                        last = nc.tensor.matmul(ps_o[:, b, :], prT[:, c, b * P:(b + 1) * P], values[:, c, 0:D],
                                                start=c == 0, stop=c == NB - 1)
                last.then_inc(gen_pe, 1)

            pe.wait_ge(redo_set, 1)
            with pe.If(pe.value_load(redo_i[0:1, 0:1], min_val=0, max_val=1)):
                with pe.Fori(0, B) as g:
                    pe.wait_ge(gen_in, g * 32 + 32)
                    pe.wait_ge(gen_dve, done(GEN_DVE, g, "adj"))
                    for c in range(NB):
                        for b in range(NB):
                            last = nc.tensor.transpose(ps_adjT[:, c, b * P:(b + 1) * P], adj_bf[:, b, c * P:(c + 1) * P], ident_bf[:, :])
                    last.then_inc(gen_pe, 1)
                    for l in range(2):
                        transpose_x(g, l)
                        for b in range(NB):
                            last = nc.tensor.matmul(ps_h[:, b * HC:(b + 1) * HC], xT[:, b * P:(b + 1) * P], w_ext[:, l, :],
                                                    start=True, stop=True)
                        last.then_inc(gen_pe, 1)
                        nc.tensor.matmul(ps_d[:, 0:N], wd_rep[:, l, :], xT[:, :], start=True, stop=True).then_inc(gen_pe, 1)
                        pe.wait_ge(gen_act, done(GEN_ACT, g, f"exp{l}"))
                        for c in range(NB):
                            for b in range(NB):
                                last = nc.tensor.transpose(ps_p[:, c, b * P:(b + 1) * P], pr[:, b, c * P:(c + 1) * P], ident[:, :])
                        last.then_inc(gen_pe, 1)
                        pe.wait_ge(gen_act, done(GEN_ACT, g, f"pT{l}"))
                        aggregate(h)
                    transpose_x(g, 2)
                    pe.wait_ge(gen_dve, done(GEN_DVE, g, "xTa"))
                    for r in range(R):
                        if r:
                            pe.wait_ge(gen_act, done(GEN_ACT, g, f"score{r - 1}"))
                        for c in range(NB):
                            last = nc.tensor.matmul(ps_p[:, c, :], xTa[:, r, c * P:(c + 1) * P], xT[:, :], start=True, stop=True)
                        last.then_inc(gen_pe, 1)
                    pe.wait_ge(gen_dve, done(GEN_DVE, g, "sum3"))
                    aggregate(xg)
                    transpose_x(g, 3)
                    for b in range(NB):
                        last = nc.tensor.matmul(ps_xw[:, b, :], xT[:, b * P:(b + 1) * P], w3[:, :, :].rearrange("p r d -> p (r d)"),
                                                start=True, stop=True)
                    last.then_inc(gen_pe, 1)
                    pe.wait_ge(gen_act, done(GEN_ACT, g, "xw"))
                    pe.wait_ge(gen_dve, done(GEN_DVE, g, "rel3"))
                    for b in range(NB):
                        for r in range(R):
                            for c in range(NB):
                                last = nc.tensor.matmul(ps_o[:, b, :], rel[:, r, c, b * P:(b + 1) * P], xw[:, c, r * D:(r + 1) * D],
                                                        start=r == 0 and c == 0, stop=r == R - 1 and c == NB - 1)
                    last.then_inc(gen_pe, 1)

_INS = ["x", "adj", "L0_gnn_W", "L0_gnn_a_src", "L0_gnn_a_dst", "L1_gnn_W", "L1_gnn_a", "L2_gnn_a0", "L2_gnn_a1",
        "L2_gnn_a2", "L2_gnn_a3", "L2_gnn_bias", "L3_gnn_adj", "L3_gnn_weight", "L3_gnn_bias"]


def kernel(**inputs):
    import numpy as np
    import concourse.bacc as bacc
    from concourse.bass_utils import run_bass_kernel_spmd

    nc = bacc.Bacc("TRN2", target_bir_lowering=False, num_devices=1)
    arrays, args = {}, []
    for name in _INS:
        a = np.ascontiguousarray(inputs[name])
        arrays[f"in_{name}"] = a
        args.append(nc.dram_tensor(f"in_{name}", a.shape, mybir.dt.from_np(a.dtype), kind="ExternalInput").ap())
    shape = np.shape(inputs["x"])
    args.append(nc.dram_tensor("out", shape, F32, kind="ExternalOutput").ap())
    res_gnn_kernel(nc, *args)
    r = run_bass_kernel_spmd(nc, [arrays], core_ids=[0])
    return r.results[0]["out"]
```

```python
from contextlib import ExitStack

import concourse.bass as bass
from concourse import mybir

P = 128
SLOPE = 0.2
EPS = 1e-5
ALU = mybir.AluOpType
ACT = mybir.ActivationFunctionType
AX = mybir.AxisListType
F32 = mybir.dt.float32
BF16 = mybir.dt.bfloat16
F16 = mybir.dt.float16
BIG = 1e30
UP = 4096.0
LOGIT_CAP = 24.0
TINY = 1e-30
I32 = mybir.dt.int32

GEN_PE = ["adjT"]
for _l in "01":
    GEN_PE += [n + _l for n in ("xT", "h", "dst", "pT", "out")]
GEN_PE += ["xT2"] + [f"score{r}" for r in range(4)] + ["out2", "xT3", "xw", "out3"]
GEN_ACT = ["adjT"]
for _l in "01":
    GEN_ACT += [n + _l for n in ("xT", "h", "sum", "exp", "pT")]
GEN_ACT += ["xT2"]
for _r in "0123":
    GEN_ACT += ["score" + _r, "sigmoid" + _r]
GEN_ACT += ["xT3", "xw"]
LN_STEPS = ["res", "stats", "aggr", "var", "norm"]
GEN_DVE = ["adj", "edge", "none0", "none1"]
for _l in "01":
    GEN_DVE += [n + _l for n in ("leaky", "keep", "mask", "max", "negmax", "rinv")] + [n + _l for n in LN_STEPS]
GEN_DVE += ["xTa"]
for _r in "0123":
    GEN_DVE += ["leaky2" + _r, "pick" + _r] + (["sum" + _r] if _r != "0" else [])
GEN_DVE += ["add2"] + [n + "2" for n in LN_STEPS] + ["rel3", "add3"] + [n + "3" for n in LN_STEPS]
GEN_POOL = [f"pow{l}" for l in range(4)]



def done(steps, g, name):
    return g * len(steps) + steps.index(name) + 1


U = 8
K = 4
H = U // K
FAST_PE = ["maskT"] + [n + l for l in "01" for n in ("xT", "h", "spread_d", "spread_s", "out")] + ["xT2", "score", "out2", "agg", "out3"]
FAST_ACT = ["maskT"] + [n + l for l in "01" for n in ("xT", "h", "factors", "scale", "grow", "norm")]
FAST_ACT += ["xT2", "xTa", "sigmoid", "norm2", "high", "agg", "norm3"]
FAST_LN = ["res", "stats", "aggr", "var", "center"]
FAST_DVE = ["raw", "mask", "off"] + [n + l for l in "01" for n in ["dmax", "shift", "weight", "rsum", "rinv"] + FAST_LN]
FAST_DVE += ["alpha"] + [n + "2" for n in FAST_LN] + ["low"] + [n + "3" for n in FAST_LN]
FAST_POOL = ["pow0", "pow1", "bias2", "pow2", "bias3", "pow3"]
WHOLE = tuple(n + l for n in ("factors", "shift", "rsum", "rinv", "var", "center", "pow") for l in "0123")
LAG = 5.0
ATTENTION = {
    "pe": [("transpose", 0.0), ("project", 1.3), ("spread_d", 2.6), ("spread_s", 3.8), ("output", 8.0)],
    "act": [("copy_xT", 0.6), ("copy_h", 2.2), ("factors", 4.6), ("grow", 5.4), ("normalize", 12.5)],
    "dve": [("largest", 3.5), ("shifts", 4.3), ("weights", 6.0), ("residual", 9.0), ("moments", 10.0), ("centers", 12.2)],
    "pool": [("pow", 11.0), ("odd", 11.1)],
}
TIMES = [
    (2.0, {"pe": [("mask", 1.0)], "act": [("mask", 1.5)], "dve": [("mask", 0.0), ("off", 3.0)], "pool": []}),
    (13.5, ATTENTION),
    (13.5, ATTENTION),
    (12.0, {
        "pe": [("transpose", 0.0), ("score", 1.8), ("output", 6.5)],
        "act": [("copy_xT", 0.6), ("copy_xTa", 0.9), ("sigmoid", 3.2), ("normalize", 11.0)],
        "dve": [("alpha", 5.0), ("residual", 7.5), ("moments", 8.5), ("centers", 10.7)],
        "pool": [("bias", 0.1), ("pow", 9.5)],
    }),
    (10.0, {
        "pe": [("gather", 1.6), ("output", 3.5)],
        "act": [("high", 0.0), ("copy_gathered", 2.5), ("normalize", 8.5)],
        "dve": [("low", 0.6), ("residual", 4.7), ("moments", 5.5), ("centers", 8.0)],
        "pool": [("bias", 0.1), ("pow", 6.8)],
    }),
]


def order(engine):
    found = []
    for k in range(K):
        start = k * LAG
        for l, (length, steps) in enumerate(TIMES):
            found += [(start + time, k, name, l - 1) for name, time in steps[engine]]
            start += length
    return [(name, l, k) for _, k, name, l in sorted(found, key=lambda step: step[:2])]


def total(steps):
    return sum(1 if n in WHOLE else H for n in steps)


def at(steps, t, name, u):
    before = total(steps[:steps.index(name)])
    return t * total(steps) + before + (0 if name in WHOLE else u % H) + 1


def res_gnn_kernel(nc, x, adj, W0, a_src0, a_dst0, W1, a1, a2_0, a2_1, a2_2, a2_3, bias2, adj3, W3, bias3, out):
    B, N, D = x.shape
    NB = N // P
    R = W3.shape[0]
    assert D == P and NB == 2 and R == 4
    HC = D + 2

    x_blocks = x.rearrange("g (b p) d -> g p b d", p=P)
    out_blocks = out.rearrange("g (b p) d -> g p b d", p=P)
    adj_blocks = adj.rearrange("g (b p) n -> g p b n", p=P)

    with ExitStack() as ctx:
        def sb(name, shape, dt=F32):
            return ctx.enter_context(nc.sbuf_tensor(name, shape, dt))

        def bank(name, shape, dt=F32):
            return ctx.enter_context(nc.psum_tensor(name, shape, dt))

        def sem(name):
            return ctx.enter_context(nc.semaphore(name))

        zero = sb("zero", [P, P])
        ident = sb("ident", [P, P])
        ident_bf = sb("ident_bf", [P, P], BF16)
        minus_half = sb("minus_half", [P, H, NB])
        w_nat = sb("w_nat", [P, 2, D])
        a_col = sb("a_col", [P, 2, 2])
        a_rep = sb("a_rep", [P, 2, 2, P])
        w_ext = sb("w_ext", [P, 2, HC])
        wd_rep = sb("wd_rep", [P, 2, P])
        a2 = sb("a2", [P, 4])
        w3 = sb("w3", [P, R, D])
        bias = sb("bias", [P, 2, NB, D])

        banks = bank("banks", [P, 8, 512])
        ps = [banks[:, u, :] for u in range(U)]
        ps_adjT = banks[:, 0, 0:NB * N // 2].bitcast(BF16).rearrange("p (b n) -> p b n", b=NB)
        ps_xT = banks[:, 1, :]
        ps_h = banks[:, 2, :]
        ps_d = banks[:, 3, :]
        ps_p = banks[:, 4, :].rearrange("p (b n) -> p b n", b=NB)
        ps_o = banks[:, 5, :].rearrange("p (b n) -> p b n", n=D)
        ps_xw = banks[:, 6:8, :]

        def each(name, shape, dt=F32):
            return [sb(f"{name}_{u}", shape, dt) for u in range(U)]

        wait_carrier = sb("wait_carrier", [P, 1])
        ws_rep = sb("ws_rep", [P, 2, P])
        big_ident = sb("big_ident", [P, P], BF16)
        x_in = each("x_in", [P, NB, D])
        adj_in = each("adj_in", [P, NB, N], I32)
        raw = each("raw", [P, NB, N], BF16)
        mask = each("mask", [P, NB, N], BF16)
        maskT = each("maskT", [P, NB, N], BF16)
        off = each("off", [P, NB, N], BF16)
        xs = each("xs", [P, NB, D])
        x_out = each("x_out", [P, NB, D])
        xb = each("xb", [P, NB, D])
        fxT = each("fxT", [P, N])
        fxTa = each("fxTa", [P, N])
        fh_all = sb("fh_all", [P, U, NB, HC + 2])
        fh = [fh_all[:, u, :, :] for u in range(U)]
        vals = each("vals", [P, NB, D + 1])
        dmax = sb("dmax", [P, U])
        dmax8 = sb("dmax8", [P, U])
        shift = sb("shift", [P, U, NB])
        fac = sb("fac", [P, 2, U, NB])
        grow = each("grow", [P, N])
        wgt_all = sb("wgt_all", [P, U, NB, N])
        wgt = [wgt_all[:, u, :, :] for u in range(U)]
        sg_all = sb("sg_all", [P, U, 2, NB, N])
        sg = [sg_all[:, u, :, :, :] for u in range(U)]
        odd = sb("odd", [P, NB, N])
        odd_sq = sb("odd_sq", [P, NB, N])
        hi = each("hi", [P, NB, D], F16)
        lo = each("lo", [P, NB, D], F16)
        aggT = fxT
        frow = sb("frow", [P, U, NB])
        finv = sb("finv", [P, U, NB])
        fmv = sb("fmv", [P, U, NB, 2])
        fcenter = sb("fcenter", [P, U, NB])
        fvar = sb("fvar", [P, U, NB])
        frstd = sb("frstd", [P, U, NB])
        fres = each("fres", [P, NB, D])
        fstats = each("fstats", [P, NB, 6])
        xg = xs[0]
        adj_i = adj_in[0]
        adj_bf = raw[0]
        adjT = maskT[0]
        xT = fxT[0]
        h = fh[0][:, :, 0:HC]
        pages = sg_all[:, :, :, :, :].rearrange("p u k b n -> p (u k) b n")
        none = pages[:, 0:2, :, :]
        rel = pages[:, 2:6, :, :]
        e, em, pr, prT, sig, pick, edge = (pages[:, 6 + k, :, :] for k in range(7))
        xw = pages[:, 13:15, :, :].rearrange("p k b n -> p k (b n)")
        xTa = wgt_all[:, 0:2, :, :].rearrange("p k b n -> p (k b) n")
        res = fres[0]
        mx = sb("mx", [P, NB])
        neg_mx = sb("neg_mx", [P, NB])
        row_sum = sb("row_sum", [P, NB])
        row_inv = sb("row_inv", [P, NB])
        stats = sb("stats", [P, NB, 6])
        mv = sb("mv", [P, NB, 2])
        var_eps = sb("var_eps", [P, NB])
        rstd = sb("rstd", [P, NB])

        odd_sum = sb("odd_sum", [P, NB, N])
        logit_max = sb("logit_max", [P, K, H, NB, 2])
        logit_min = sb("logit_min", [P, K, H, NB, 2])
        row_min = sb("row_min", [P, K, H, NB])
        bad = sb("bad", [P, 9])
        ones_col = sb("ones_col", [P, 1])
        redo_f = sb("redo_f", [1, 1])
        redo_i = sb("redo_i", [1, 1], I32)

        weights_in = sem("weights_in")
        fast_adj_in = [sem(f"fast_adj_in_{u}") for u in range(U)]
        fast_x_in = [sem(f"fast_x_in_{u}") for u in range(U)]
        fast_pe = [sem(f"fast_pe_{k}") for k in range(K)]
        fast_act = [sem(f"fast_act_{k}") for k in range(K)]
        fast_dve = [sem(f"fast_dve_{k}") for k in range(K)]
        fast_pool = [sem(f"fast_pool_{k}") for k in range(K)]
        fast_stored = [sem(f"fast_stored_{k}") for k in range(K)]
        met_set = sem("met_set")
        odd_step = sem("odd_step")
        bad_step = sem("bad_step")
        bad_summed = sem("bad_summed")
        redo_set = sem("redo_set")
        zero_set = sem("zero_set")
        ident_set = sem("ident_set")
        ident_bf_set = sem("ident_bf_set")
        a_rep_set = sem("a_rep_set")
        wT_made = sem("wT_made")
        w_ext_set = sem("w_ext_set")
        gen_in = sem("gen_in")
        gen_pe = sem("gen_pe")
        gen_act = sem("gen_act")
        gen_dve = sem("gen_dve")
        gen_pool = sem("gen_pool")
        gen_out = sem("gen_out")

        loads = [
            (w_nat[:, 0, :], W0), (w_nat[:, 1, :], W1),
            (a_col[:, 0, 0:1], a_src0.rearrange("(p a) -> p a", a=1)),
            (a_col[:, 0, 1:2], a_dst0.rearrange("(p a) -> p a", a=1)),
            (a_col[:, 1, 0:1], a1[0:D].rearrange("(p a) -> p a", a=1)),
            (a_col[:, 1, 1:2], a1[D:2 * D].rearrange("(p a) -> p a", a=1)),
            (a2[:, 0:1], a2_0), (a2[:, 1:2], a2_1), (a2[:, 2:3], a2_2), (a2[:, 3:4], a2_3),
            (w3[:, :, :], W3.rearrange("r d o -> d r o")),
        ]
        for k, bb in ((0, bias2), (1, bias3)):
            for b in range(NB):
                loads.append((bias[:, k, b, :], bb.rearrange("(a d) -> a d", a=1).to_broadcast([P, D])))
        WEIGHTS = 16 * (len(loads) - U)
        T = B // U

        block = ctx.enter_context(nc.Block())

        @block.sync
        def _(sp):
            for n, (dst, src) in enumerate(loads):
                sp.dma_start(dst, src).then_inc(weights_in if n < len(loads) - U else fast_stored[n % K], 16)

            def fast_load_adj(t, u):
                sp.dma_start(adj_in[u][:, :, :], adj_blocks[t * U + u]).then_inc(fast_adj_in[u], 16)

            def fast_load_x(t, u):
                sp.dma_start(x_in[u][:, :, :], x_blocks[t * U + u]).then_inc(fast_x_in[u], 16)

            def fast_store(t, u):
                sp.wait_ge(fast_act[u // H], at(FAST_ACT, t, "norm3", u))
                sp.dma_start(out_blocks[t * U + u], x_out[u][:, :, :]).then_inc(fast_stored[u // H], 16)

            for u in range(U):
                fast_load_adj(0, u)
                fast_load_x(0, u)
            with sp.Fori(0, T - 1) as t:
                for u in range(U):
                    sp.wait_ge(fast_dve[u // H], at(FAST_DVE, t, "raw", u))
                    fast_load_adj(t + 1, u)
                for u in range(U):
                    sp.wait_ge(fast_dve[u // H], at(FAST_DVE, t, "res0", u))
                    fast_load_x(t + 1, u)
                for u in range(U):
                    fast_store(t, u)
            for u in range(U):
                fast_store(T - 1, u)
            for k in range(K):
                sp.wait_ge(fast_stored[k], 16 * H * (T + 1))

            sp.wait_ge(redo_set, 1)
            with sp.If(sp.value_load(redo_i[0:1, 0:1], min_val=0, max_val=1)):
                def load(g):
                    sp.dma_start(xg[:, :, :], x_blocks[g]).then_inc(gen_in, 16)
                    sp.dma_start(adj_i[:, :, :], adj_blocks[g]).then_inc(gen_in, 16)

                def store(g):
                    sp.wait_ge(gen_dve, done(GEN_DVE, g, "norm3"))
                    sp.dma_start(out_blocks[g], xg[:, :, :]).then_inc(gen_out, 16)

                load(0)
                with sp.Fori(0, B - 1) as g:
                    store(g)
                    sp.wait_ge(gen_out, g * 16 + 16)
                    load(g + 1)
                store(B - 1)
                sp.wait_ge(gen_out, B * 16)

        @block.gpsimd
        def _(pool):
            nc.gpsimd.memset(zero[:, :], 0.0).then_inc(zero_set, 1)
            nc.gpsimd.memset(minus_half[:, :, :], -0.5).then_inc(ident_set, 1)
            pool.wait_ge(zero_set, 1)
            nc.gpsimd.affine_select(out=ident[:, :], in_=zero[:, :], compare_op=ALU.not_equal, fill=1.0,
                                    base=0, pattern=[[-1, P]], channel_multiplier=1).then_inc(ident_set, 1)
            nc.gpsimd.memset(odd_sum[:, :, :], 0.0).then_inc(ident_set, 1)
            pool.wait_ge(ident_set, 3)
            with pool.Fori(0, T) as t:
                looked = 0
                for step, l, k in order("pool"):
                    if step == "bias":
                        for u in range(k * H, (k + 1) * H):
                            pool.wait_ge(fast_act[k], at(FAST_ACT, t, f"norm{l - 1}", u))
                            nc.gpsimd.tensor_tensor(xb[u][:, :, :], xs[u][:, :, :], bias[:, l - 2, :, :], ALU.add).then_inc(fast_pool[k], 1)
                    elif step == "pow":
                        pool.wait_ge(fast_dve[k], at(FAST_DVE, t, f"var{l}", k * H))
                        nc.gpsimd.tensor_tensor(frstd[:, k * H:(k + 1) * H, :], fvar[:, k * H:(k + 1) * H, :], minus_half[:, :, :],
                                                ALU.pow).then_inc(fast_pool[k], 1)
                    else:
                        u = k * H + l
                        pool.wait_ge(fast_dve[k], at(FAST_DVE, t, "mask", u))
                        nc.gpsimd.tensor_tensor(odd[:, :, :], raw[u][:, :, :], mask[u][:, :, :], ALU.subtract).then_inc(odd_step, 1)
                        pool.wait_ge(odd_step, t * (3 * U) + 3 * looked + 1)
                        nc.gpsimd.tensor_tensor(odd_sq[:, :, :], odd[:, :, :], odd[:, :, :], ALU.mult).then_inc(odd_step, 1)
                        pool.wait_ge(odd_step, t * (3 * U) + 3 * looked + 2)
                        nc.gpsimd.tensor_tensor(odd_sum[:, :, :], odd_sum[:, :, :], odd_sq[:, :, :], ALU.add).then_inc(odd_step, 1)
                        looked += 1

            pool.wait_ge(redo_set, 1)
            with pool.If(pool.value_load(redo_i[0:1, 0:1], min_val=0, max_val=1)):
                with pool.Fori(0, B) as g:
                    for l in range(4):
                        pool.wait_ge(gen_dve, done(GEN_DVE, g, f"var{l}"))
                        nc.gpsimd.tensor_tensor(rstd[:, :], var_eps[:, :], minus_half[:, 0, :], ALU.pow).then_inc(gen_pool, 1)

        @block.scalar
        def _(act):
            act.wait_ge(met_set, 3 + U)
            with act.Fori(0, T) as t:
                def transposed_mask(l, k):
                    for u in range(k * H, (k + 1) * H):
                        act.wait_ge(fast_pe[k], at(FAST_PE, t, "maskT", u))
                        nc.scalar.copy(maskT[u][:, :, :], ps[u][:, 0:N].bitcast(BF16).rearrange("p (b n) -> p b n", b=NB)).then_inc(fast_act[k], 1)

                def copy_xT(l, k):
                    for u in range(k * H, (k + 1) * H):
                        act.wait_ge(fast_pe[k], at(FAST_PE, t, f"xT{l}", u))
                        nc.scalar.copy(fxT[u][:, :], ps[u][:, 0:N]).then_inc(fast_act[k], 1)

                def copy_h(l, k):
                    for u in range(k * H, (k + 1) * H):
                        act.wait_ge(fast_pe[k], at(FAST_PE, t, f"h{l}", u))
                        nc.scalar.copy(fh[u][:, :, 1:1 + HC], ps[u][:, 0:NB * HC].rearrange("p (b c) -> p b c", b=NB)).then_inc(fast_act[k], 1)

                def factors(l, k):
                    team = range(k * H, (k + 1) * H)
                    half = slice(k * H, (k + 1) * H)
                    act.wait_ge(fast_dve[k], at(FAST_DVE, t, f"shift{l}", team[0]))
                    nc.scalar.activation(fac[:, 0, half, :], shift[:, half, :], ACT.Exp)
                    nc.scalar.activation(fac[:, 1, half, :], shift[:, half, :], ACT.Exp, scale=SLOPE - 1).then_inc(fast_act[k], 1)
                    for u in team:
                        act.wait_ge(fast_act[k], at(FAST_ACT, t, f"factors{l}", u))
                        for c in range(NB):
                            last = nc.scalar.activation(vals[u][:, c, :], fh[u][:, c, 0:D + 1], ACT.Copy, scale=fac[:, 0, u, c:c + 1])
                        last.then_inc(fast_act[k], 1)

                def grow_rows(l, k):
                    for u in range(k * H, (k + 1) * H):
                        act.wait_ge(fast_pe[k], at(FAST_PE, t, f"spread_s{l}", u))
                        nc.scalar.activation(grow[u][:, :], ps[u][:, 0:N], ACT.Exp, bias=dmax8[:, u:u + 1], scale=1 - SLOPE).then_inc(fast_act[k], 1)

                def copy_xTa(l, k):
                    for u in range(k * H, (k + 1) * H):
                        nc.scalar.activation(fxTa[u][:, :], ps[u][:, 0:N], ACT.Copy, scale=a2[:, 0:1]).then_inc(fast_act[k], 1)

                def sigmoids(l, k):
                    for u in range(k * H, (k + 1) * H):
                        act.wait_ge(fast_pe[k], at(FAST_PE, t, "score", u))
                        for n, slope in enumerate((1.0, SLOPE)):
                            last = nc.scalar.activation(sg[u][:, n, :, :], ps[u].rearrange("p (b n) -> p b n", b=NB), ACT.Sigmoid, scale=slope)
                        last.then_inc(fast_act[k], 1)

                def high_part(l, k):
                    for u in range(k * H, (k + 1) * H):
                        act.wait_ge(fast_act[k], at(FAST_ACT, t, "norm2", u))
                        nc.scalar.activation(hi[u][:, :, :], xs[u][:, :, :], ACT.Copy, scale=UP).then_inc(fast_act[k], 1)

                def copy_gathered(l, k):
                    for u in range(k * H, (k + 1) * H):
                        act.wait_ge(fast_pe[k], at(FAST_PE, t, "agg", u))
                        nc.scalar.activation(aggT[u][:, :], ps[u][:, 0:N], ACT.Copy, scale=1 / UP).then_inc(fast_act[k], 1)

                def normalize(l, k):
                    dst = x_out if l == 3 else xs
                    for u in range(k * H, (k + 1) * H):
                        act.wait_ge(fast_dve[k], at(FAST_DVE, t, f"center{l}", u))
                        if l == 3:
                            act.wait_ge(fast_stored[k], t * (16 * H) + 16 * H)
                        for b in range(NB):
                            last = nc.scalar.activation(dst[u][:, b, :], fres[u][:, b, :], ACT.Identity, bias=fcenter[:, u, b:b + 1],
                                                        scale=frstd[:, u, b:b + 1])
                        last.then_inc(fast_act[k], 1)

                steps = {"mask": transposed_mask, "copy_xT": copy_xT, "copy_h": copy_h, "factors": factors, "grow": grow_rows,
                         "copy_xTa": copy_xTa, "sigmoid": sigmoids, "high": high_part, "copy_gathered": copy_gathered,
                         "normalize": normalize}
                for step, l, k in order("act"):
                    steps[step](l, k)

            act.wait_ge(redo_set, 1)
            with act.If(act.value_load(redo_i[0:1, 0:1], min_val=0, max_val=1)):
                with act.Fori(0, B) as g:
                    act.wait_ge(gen_pe, done(GEN_PE, g, "adjT"))
                    nc.scalar.copy(adjT[:, :, :], ps_adjT[:, :, :]).then_inc(gen_act, 1)
                    for l in range(2):
                        act.wait_ge(gen_pe, done(GEN_PE, g, f"xT{l}"))
                        nc.scalar.copy(xT[:, :], ps_xT[:, 0:N]).then_inc(gen_act, 1)
                        act.wait_ge(gen_pe, done(GEN_PE, g, f"h{l}"))
                        nc.scalar.copy(h[:, :, :], ps_h[:, 0:NB * HC].rearrange("p (b c) -> p b c", b=NB)).then_inc(gen_act, 1)
                        act.wait_ge(gen_pe, done(GEN_PE, g, f"dst{l}"))
                        act.wait_ge(gen_act, done(GEN_ACT, g, f"h{l}"))
                        for b in range(NB):
                            last = nc.scalar.activation(e[:, b, :], ps_d[:, 0:N], ACT.Identity, bias=h[:, b, D:D + 1])
                        last.then_inc(gen_act, 1)
                        act.wait_ge(gen_dve, done(GEN_DVE, g, f"negmax{l}"))
                        for b in range(NB):
                            last = nc.scalar.activation(pr[:, b, :], em[:, b, :], ACT.Exp, bias=neg_mx[:, b:b + 1],
                                                        accum_out=row_sum[:, b:b + 1])
                        last.then_inc(gen_act, 1)
                        act.wait_ge(gen_pe, done(GEN_PE, g, f"pT{l}"))
                        nc.scalar.copy(prT[:, :, :], ps_p[:, :, :]).then_inc(gen_act, 1)
                    act.wait_ge(gen_pe, done(GEN_PE, g, "xT2"))
                    nc.scalar.copy(xT[:, :], ps_xT[:, 0:N]).then_inc(gen_act, 1)
                    for r in range(R):
                        act.wait_ge(gen_pe, done(GEN_PE, g, f"score{r}"))
                        nc.scalar.copy(e[:, :, :], ps_p[:, :, :]).then_inc(gen_act, 1)
                        act.wait_ge(gen_dve, done(GEN_DVE, g, f"leaky2{r}"))
                        if r:
                            act.wait_ge(gen_dve, done(GEN_DVE, g, f"pick{r - 1}"))
                        nc.scalar.activation(sig[:, :, :], em[:, :, :], ACT.Sigmoid).then_inc(gen_act, 1)
                    act.wait_ge(gen_pe, done(GEN_PE, g, "xT3"))
                    nc.scalar.copy(xT[:, :], ps_xT[:, 0:N]).then_inc(gen_act, 1)
                    act.wait_ge(gen_pe, done(GEN_PE, g, "xw"))
                    for b in range(NB):
                        last = nc.scalar.copy(xw[:, b, :], ps_xw[:, b, :])
                    last.then_inc(gen_act, 1)

        @block.vector
        def _(dve):
            dve.wait_ge(ident_set, 2)
            nc.vector.tensor_copy(ident_bf[:, :], ident[:, :]).then_inc(ident_bf_set, 1)
            nc.vector.tensor_scalar(big_ident[:, :], ident[:, :], BIG, None, ALU.mult).then_inc(ident_bf_set, 1)
            nc.vector.memset(ones_col[:, :], 1.0).then_inc(ident_bf_set, 1)
            nc.vector.memset(logit_max[:, :, :, :, :], 0.0).then_inc(met_set, 1)
            nc.vector.memset(logit_min[:, :, :, :, :], 0.0).then_inc(met_set, 1)
            nc.vector.memset(row_min[:, :, :, :], 1.0).then_inc(met_set, 1)
            for u in range(U):
                nc.vector.memset(fh[u][:, :, 0:1], 1.0).then_inc(met_set, 1)
            dve.wait_ge(met_set, 3 + U)
            dve.wait_ge(weights_in, WEIGHTS)
            for k in range(K):
                dve.wait_ge(fast_stored[k], 16 * H)
            for l in range(2):
                for k in range(2):
                    nc.vector.tensor_scalar(a_rep[:, l, k, :], zero[:, :], a_col[:, l, k:k + 1], None, ALU.add).then_inc(a_rep_set, 1)
            for l in range(2):
                dve.wait_ge(wT_made, l + 1)
                nc.vector.tensor_copy(w_ext[:, l, :], ps_h[:, 0:HC])
                nc.vector.tensor_copy(ws_rep[:, l, :], ps_h[:, 256:256 + P])
                nc.vector.tensor_copy(wd_rep[:, l, :], ps_h[:, 384:384 + P]).then_inc(w_ext_set, 1)

            with dve.Fori(0, T) as t:
                def make_masks(l, k):
                    team = range(k * H, (k + 1) * H)
                    for u in team:
                        dve.wait_ge(fast_adj_in[u], t * 16 + 16)
                        nc.vector.tensor_copy(raw[u][:, :, :], adj_in[u][:, :, :]).then_inc(fast_dve[k], 1)
                    for u in team:
                        dve.wait_ge(fast_dve[k], at(FAST_DVE, t, "raw", u))
                        nc.vector.tensor_scalar(mask[u][:, :, :], raw[u][:, :, :], 0.0, None, ALU.not_equal).then_inc(fast_dve[k], 1)

                def off_graph(l, k):
                    for u in range(k * H, (k + 1) * H):
                        dve.wait_ge(fast_act[k], at(FAST_ACT, t, "maskT", u))
                        nc.vector.tensor_scalar(off[u][:, :, :], maskT[u][:, :, :], -1.0, None, ALU.add).then_inc(fast_dve[k], 1)

                def largest(l, k):
                    for u in range(k * H, (k + 1) * H):
                        dve.wait_ge(fast_pe[k], at(FAST_PE, t, f"spread_d{l}", u))
                        nc.vector.tensor_reduce(dmax[:, u:u + 1], ps[u][:, N:2 * N], AX.X, ALU.max).then_inc(fast_dve[k], 1)

                def shifts(l, k):
                    team = range(k * H, (k + 1) * H)
                    half = slice(k * H, (k + 1) * H)
                    parts = fh_all[:, half, :, D + 1:D + 3]
                    dve.wait_ge(fast_act[k], at(FAST_ACT, t, f"h{l}", team[-1]))
                    nc.vector.tensor_tensor(logit_max[:, k, :, :, :], logit_max[:, k, :, :, :], parts, ALU.max)
                    nc.vector.tensor_tensor(logit_min[:, k, :, :, :], logit_min[:, k, :, :, :], parts, ALU.min)
                    dve.wait_ge(fast_dve[k], at(FAST_DVE, t, f"dmax{l}", team[-1]))
                    nc.vector.tensor_tensor(shift[:, half, :], fh_all[:, half, :, D + 2],
                                            dmax[:, half].rearrange("p (u a) -> p u a", a=1).to_broadcast([P, H, NB]), ALU.subtract)
                    nc.vector.tensor_scalar(dmax8[:, half], dmax[:, half], 1 - SLOPE, None, ALU.mult).then_inc(fast_dve[k], 1)

                def weights(l, k):
                    for u in range(k * H, (k + 1) * H):
                        dve.wait_ge(fast_act[k], at(FAST_ACT, t, f"grow{l}", u))
                        for c in range(NB):
                            last = nc.vector.scalar_tensor_tensor(out=wgt[u][:, c, :], in0=grow[u][:, :], scalar=fac[:, 1, u, c:c + 1],
                                                                  in1=maskT[u][:, c, :], op0=ALU.max, op1=ALU.mult)
                        last.then_inc(fast_dve[k], 1)

                def alpha(l, k):
                    for u in range(k * H, (k + 1) * H):
                        dve.wait_ge(fast_act[k], at(FAST_ACT, t, "sigmoid", u))
                        nc.vector.tensor_tensor(wgt[u][:, :, :], sg[u][:, 0, :, :], sg[u][:, 1, :, :], ALU.max).then_inc(fast_dve[k], 1)

                def low_part(l, k):
                    for u in range(k * H, (k + 1) * H):
                        dve.wait_ge(fast_act[k], at(FAST_ACT, t, "high", u))
                        nc.vector.scalar_tensor_tensor(out=lo[u][:, :, :], in0=xs[u][:, :, :], scalar=UP, in1=hi[u][:, :, :],
                                                       op0=ALU.mult, op1=ALU.subtract).then_inc(fast_dve[k], 1)

                def residual(l, k):
                    team = range(k * H, (k + 1) * H)
                    half = slice(k * H, (k + 1) * H)
                    if l >= 2:
                        for u in team:
                            dve.wait_ge(fast_pool[k], at(FAST_POOL, t, f"bias{l}", u))
                            dve.wait_ge(fast_pe[k], at(FAST_PE, t, f"out{l}", u))
                            nc.vector.tensor_tensor(fres[u][:, :, :], ps[u][:, 0:NB * D].rearrange("p (b c) -> p b c", b=NB), xb[u][:, :, :],
                                                    ALU.add).then_inc(fast_dve[k], 1)
                        return
                    x_l = x_in if l == 0 else xs
                    sums = banks[:, half, 0:NB * (D + 1)].rearrange("p u (b c) -> p u b c", b=NB)
                    dve.wait_ge(fast_pe[k], at(FAST_PE, t, f"out{l}", team[-1]))
                    nc.vector.tensor_scalar(frow[:, half, :], sums[:, :, :, 0], TINY, None, ALU.max).then_inc(fast_dve[k], 1)
                    dve.wait_ge(fast_dve[k], at(FAST_DVE, t, f"rsum{l}", team[0]))
                    nc.vector.tensor_tensor(row_min[:, k, :, :], row_min[:, k, :, :], frow[:, half, :], ALU.min)
                    nc.vector.reciprocal(finv[:, half, :], frow[:, half, :]).then_inc(fast_dve[k], 1)
                    dve.wait_ge(fast_dve[k], at(FAST_DVE, t, f"rinv{l}", team[0]))
                    for u in team:
                        for b in range(NB):
                            last = nc.vector.scalar_tensor_tensor(out=fres[u][:, b, :], in0=sums[:, u - k * H, b, 1:D + 1], scalar=finv[:, u, b:b + 1],
                                                                  in1=x_l[u][:, b, :], op0=ALU.mult, op1=ALU.add)
                        last.then_inc(fast_dve[k], 1)

                def moments(l, k):
                    team = range(k * H, (k + 1) * H)
                    half = slice(k * H, (k + 1) * H)
                    for u in team:
                        dve.wait_ge(fast_dve[k], at(FAST_DVE, t, f"res{l}", u))
                        for b in range(NB):
                            last = nc.vector.bn_stats(fstats[u][:, b, :], fres[u][:, b, :])
                        last.then_inc(fast_dve[k], 1)
                    dve.wait_ge(fast_dve[k], at(FAST_DVE, t, f"stats{l}", team[-1]))
                    nc.vector.memset(wait_carrier[:, :], 0.0)
                    for u in team:
                        for b in range(NB):
                            last = nc.vector.bn_aggr(fmv[:, u, b, :], fstats[u][:, b, :])
                        last.then_inc(fast_dve[k], 1)
                    dve.wait_ge(fast_dve[k], at(FAST_DVE, t, f"aggr{l}", team[-1]))
                    nc.vector.tensor_scalar(fvar[:, half, :], fmv[:, half, :, 1], EPS, None, ALU.add).then_inc(fast_dve[k], 1)

                def centers(l, k):
                    team = range(k * H, (k + 1) * H)
                    half = slice(k * H, (k + 1) * H)
                    dve.wait_ge(fast_pool[k], at(FAST_POOL, t, f"pow{l}", team[0]))
                    nc.vector.scalar_tensor_tensor(out=fcenter[:, half, :], in0=fmv[:, half, :, 0], scalar=-1.0, in1=frstd[:, half, :],
                                                   op0=ALU.mult, op1=ALU.mult).then_inc(fast_dve[k], 1)

                steps = {"mask": make_masks, "off": off_graph, "largest": largest, "shifts": shifts, "weights": weights,
                         "alpha": alpha, "low": low_part, "residual": residual, "moments": moments, "centers": centers}
                for step, l, k in order("dve"):
                    steps[step](l, k)

            dve.wait_ge(odd_step, T * 3 * U)
            for k in range(K):
                dve.wait_ge(fast_pool[k], T * total(FAST_POOL))
                dve.wait_ge(fast_dve[k], T * total(FAST_DVE))
            nc.vector.tensor_reduce(bad[:, 0:1], odd_sum[:, :, :], AX.XY, ALU.max)
            nc.vector.tensor_reduce(bad[:, 1:2], logit_max[:, :, :, :, :].rearrange("p t h b k -> p (t h b k)"), AX.X, ALU.max)
            nc.vector.tensor_reduce(bad[:, 7:8], logit_min[:, :, :, :, :].rearrange("p t h b k -> p (t h b k)"), AX.X, ALU.min)
            nc.vector.tensor_reduce(bad[:, 2:3], row_min[:, :, :, :].rearrange("p t h b -> p (t h b)"), AX.X, ALU.min).then_inc(bad_step, 1)
            dve.wait_ge(bad_step, 1)
            nc.vector.tensor_scalar(bad[:, 3:4], bad[:, 0:1], 0.0, None, ALU.is_gt)
            nc.vector.tensor_scalar(bad[:, 4:5], bad[:, 1:2], LOGIT_CAP, None, ALU.is_gt)
            nc.vector.tensor_scalar(bad[:, 6:7], bad[:, 7:8], -LOGIT_CAP, None, ALU.is_lt)
            nc.vector.tensor_scalar(bad[:, 5:6], bad[:, 2:3], TINY, None, ALU.is_le).then_inc(bad_step, 1)
            dve.wait_ge(bad_step, 2)
            nc.vector.tensor_reduce(bad[:, 8:9], bad[:, 3:7], AX.X, ALU.max).then_inc(bad_step, 1)
            dve.wait_ge(bad_summed, 1)
            nc.vector.tensor_scalar(redo_i[:, :], ps[0][0:1, 0:1], 0.0, None, ALU.is_gt).then_inc(redo_set, 1)

            def layernorm(g, l, before):
                dve.wait_ge(gen_dve, done(GEN_DVE, g, before))
                for b in range(NB):
                    last = nc.vector.bn_stats(stats[:, b, :], res[:, b, :])
                last.then_inc(gen_dve, 1)
                dve.wait_ge(gen_dve, done(GEN_DVE, g, f"stats{l}"))
                nc.vector.memset(wait_carrier[:, :], 0.0)
                for b in range(NB):
                    last = nc.vector.bn_aggr(mv[:, b, :], stats[:, b, :])
                last.then_inc(gen_dve, 1)
                dve.wait_ge(gen_dve, done(GEN_DVE, g, f"aggr{l}"))
                nc.vector.tensor_scalar(var_eps[:, :], mv[:, :, 1], EPS, None, ALU.add).then_inc(gen_dve, 1)
                dve.wait_ge(gen_pool, done(GEN_POOL, g, f"pow{l}"))
                for b in range(NB):
                    last = nc.vector.tensor_scalar(xg[:, b, :], res[:, b, :], mv[:, b, 0:1], rstd[:, b:b + 1],
                                                   ALU.subtract, ALU.mult)
                last.then_inc(gen_dve, 1)

            dve.wait_ge(redo_set, 1)
            with dve.If(dve.value_load(redo_i[0:1, 0:1], min_val=0, max_val=1)):
                with dve.Fori(0, B) as g:
                    dve.wait_ge(gen_in, g * 32 + 32)
                    nc.vector.tensor_copy(adj_bf[:, :, :], adj_i[:, :, :]).then_inc(gen_dve, 1)
                    dve.wait_ge(gen_dve, done(GEN_DVE, g, "adj"))
                    nc.vector.tensor_scalar(edge[:, :, :], adj_bf[:, :, :], 0.0, None, ALU.not_equal).then_inc(gen_dve, 1)
                    dve.wait_ge(gen_dve, done(GEN_DVE, g, "edge"))
                    for l, neg in ((0, 1e9), (1, 9e15)):
                        nc.vector.tensor_scalar(none[:, l, :, :], edge[:, :, :], -1.0, neg, ALU.add, ALU.mult).then_inc(gen_dve, 1)
                    for l in range(2):
                        dve.wait_ge(gen_act, done(GEN_ACT, g, f"sum{l}"))
                        nc.vector.scalar_tensor_tensor(out=em[:, :, :], in0=e[:, :, :], scalar=SLOPE, in1=e[:, :, :],
                                                       op0=ALU.mult, op1=ALU.max).then_inc(gen_dve, 1)
                        dve.wait_ge(gen_dve, done(GEN_DVE, g, f"leaky{l}"))
                        nc.vector.tensor_tensor(em[:, :, :], em[:, :, :], edge[:, :, :], ALU.mult).then_inc(gen_dve, 1)
                        dve.wait_ge(gen_dve, done(GEN_DVE, g, f"keep{l}"))
                        nc.vector.tensor_tensor(em[:, :, :], em[:, :, :], none[:, l, :, :], ALU.add).then_inc(gen_dve, 1)
                        dve.wait_ge(gen_dve, done(GEN_DVE, g, f"mask{l}"))
                        nc.vector.tensor_reduce(mx[:, :], em[:, :, :], AX.X, ALU.max).then_inc(gen_dve, 1)
                        dve.wait_ge(gen_dve, done(GEN_DVE, g, f"max{l}"))
                        nc.vector.tensor_scalar(neg_mx[:, :], mx[:, :], -1.0, None, ALU.mult).then_inc(gen_dve, 1)
                        dve.wait_ge(gen_act, done(GEN_ACT, g, f"exp{l}"))
                        nc.vector.reciprocal(row_inv[:, :], row_sum[:, :]).then_inc(gen_dve, 1)
                        dve.wait_ge(gen_dve, done(GEN_DVE, g, f"rinv{l}"))
                        dve.wait_ge(gen_pe, done(GEN_PE, g, f"out{l}"))
                        for b in range(NB):
                            last = nc.vector.scalar_tensor_tensor(out=res[:, b, :], in0=ps_o[:, b, :], scalar=row_inv[:, b:b + 1],
                                                                  in1=xg[:, b, :], op0=ALU.mult, op1=ALU.add)
                        last.then_inc(gen_dve, 1)
                        layernorm(g, l, f"res{l}")
                    dve.wait_ge(gen_act, done(GEN_ACT, g, "xT2"))
                    for r in range(R):
                        last = nc.vector.tensor_scalar(xTa[:, r, :], xT[:, :], a2[:, r:r + 1], None, ALU.mult)
                    last.then_inc(gen_dve, 1)
                    for r in range(R):
                        dve.wait_ge(gen_act, done(GEN_ACT, g, f"score{r}"))
                        nc.vector.scalar_tensor_tensor(out=em[:, :, :], in0=e[:, :, :], scalar=SLOPE, in1=e[:, :, :],
                                                       op0=ALU.mult, op1=ALU.max).then_inc(gen_dve, 1)
                        dve.wait_ge(gen_act, done(GEN_ACT, g, f"sigmoid{r}"))
                        if r >= 2:
                            dve.wait_ge(gen_dve, done(GEN_DVE, g, f"sum{r - 1}"))
                        nc.vector.scalar_tensor_tensor(out=(pick if r else prT)[:, :, :], in0=adjT[:, :, :], scalar=float(r + 1),
                                                       in1=sig[:, :, :], op0=ALU.is_equal, op1=ALU.mult).then_inc(gen_dve, 1)
                        if r:
                            dve.wait_ge(gen_dve, done(GEN_DVE, g, f"pick{r}"))
                            nc.vector.tensor_tensor(prT[:, :, :], prT[:, :, :], pick[:, :, :], ALU.add).then_inc(gen_dve, 1)
                    for l in (2, 3):
                        if l == 3:
                            for r in range(R):
                                last = nc.vector.tensor_scalar(rel[:, r, :, :], adjT[:, :, :], float(r + 1), None, ALU.is_equal)
                            last.then_inc(gen_dve, 1)
                        dve.wait_ge(gen_pe, done(GEN_PE, g, f"out{l}"))
                        nc.vector.tensor_tensor(res[:, :, :], ps_o[:, 0:NB, :], xg[:, :, :], ALU.add).then_inc(gen_dve, 1)
                        dve.wait_ge(gen_dve, done(GEN_DVE, g, f"add{l}"))
                        nc.vector.tensor_tensor(res[:, :, :], res[:, :, :], bias[:, l - 2, :, :], ALU.add).then_inc(gen_dve, 1)
                        layernorm(g, l, f"res{l}")

        @block.tensor
        def _(pe):
            pe.wait_ge(ident_set, 2)
            pe.wait_ge(ident_bf_set, 3)
            pe.wait_ge(a_rep_set, 4)
            for l in range(2):
                if l:
                    pe.wait_ge(w_ext_set, l)
                nc.tensor.transpose(ps_h[:, 0:D], w_nat[:, l, :], ident[:, :])
                nc.tensor.matmul(ps_h[:, D:D + 2], w_nat[:, l, :], a_col[:, l, :], start=True, stop=True)
                nc.tensor.matmul(ps_h[:, 256:384], w_nat[:, l, :], a_rep[:, l, 0, :], start=True, stop=True)
                nc.tensor.matmul(ps_h[:, 384:512], w_nat[:, l, :], a_rep[:, l, 1, :], start=True, stop=True).then_inc(wT_made, 1)
            pe.wait_ge(w_ext_set, 2)

            with pe.Fori(0, T) as t:
                def transposed_mask(l, k):
                    for u in range(k * H, (k + 1) * H):
                        view = ps[u][:, 0:N].bitcast(BF16).rearrange("p (b n) -> p b n", b=NB)
                        pe.wait_ge(fast_dve[k], at(FAST_DVE, t, "mask", u))
                        for c in range(NB):
                            for b in range(NB):
                                last = nc.tensor.transpose(view[:, c, b * P:(b + 1) * P], mask[u][:, b, c * P:(c + 1) * P], ident_bf[:, :])
                        last.then_inc(fast_pe[k], 1)

                def transposes(l, k):
                    for u in range(k * H, (k + 1) * H):
                        x_l = x_in if l == 0 else xs
                        if l:
                            pe.wait_ge(fast_act[k], at(FAST_ACT, t, f"norm{l - 1}", u))
                        else:
                            pe.wait_ge(fast_x_in[u], t * 16 + 16)
                            pe.wait_ge(fast_act[k], at(FAST_ACT, t, "maskT", u))
                        for b in range(NB):
                            last = nc.tensor.transpose(ps[u][:, b * P:(b + 1) * P], x_l[u][:, b, :], ident[:, :])
                        last.then_inc(fast_pe[k], 1)

                def projections(l, k):
                    team = range(k * H, (k + 1) * H)
                    for u in team:
                        pe.wait_ge(fast_act[k], at(FAST_ACT, t, f"xT{l}", u))
                        for b in range(NB):
                            last = nc.tensor.matmul(ps[u][:, b * HC:(b + 1) * HC], fxT[u][:, b * P:(b + 1) * P], w_ext[:, l, :],
                                                    start=True, stop=True)
                        last.then_inc(fast_pe[k], 1)

                def spread_d(l, k):
                    for u in range(k * H, (k + 1) * H):
                        pe.wait_ge(fast_act[k], at(FAST_ACT, t, f"h{l}", u))
                        nc.tensor.matmul(ps[u][:, N:2 * N], wd_rep[:, l, :], fxT[u][:, :], start=True, stop=True).then_inc(fast_pe[k], 1)

                def spread_s(l, k):
                    for u in range(k * H, (k + 1) * H):
                        pe.wait_ge(fast_dve[k], at(FAST_DVE, t, f"dmax{l}", u))
                        nc.tensor.matmul(ps[u][:, 0:N], ws_rep[:, l, :], fxT[u][:, :], start=True, stop=True).then_inc(fast_pe[k], 1)

                def scores(l, k):
                    for u in range(k * H, (k + 1) * H):
                        pe.wait_ge(fast_act[k], at(FAST_ACT, t, "xTa", u))
                        for c in range(NB):
                            nc.tensor.matmul(ps[u][:, c * N:(c + 1) * N], fxTa[u][:, c * P:(c + 1) * P], fxT[u][:, :], start=True, stop=False)
                            last = nc.tensor.matmul(ps[u][:, c * N:(c + 1) * N], big_ident[:, :], off[u][:, c, :], start=False, stop=True)
                        last.then_inc(fast_pe[k], 1)

                def gather(l, k):
                    for u in range(k * H, (k + 1) * H):
                        pe.wait_ge(fast_dve[k], at(FAST_DVE, t, "low", u))
                        for c in range(NB):
                            for part in (hi, lo):
                                last = nc.tensor.matmul(ps[u][:, 0:N], part[u][:, c, :], maskT[u][:, c, :],
                                                        start=c == 0 and part is hi, stop=c == NB - 1 and part is lo)
                        last.then_inc(fast_pe[k], 1)

                def outputs(l, k):
                    for u in range(k * H, (k + 1) * H):
                        if l < 2:
                            pe.wait_ge(fast_act[k], at(FAST_ACT, t, f"scale{l}", u))
                            pe.wait_ge(fast_dve[k], at(FAST_DVE, t, f"weight{l}", u))
                        elif l == 2:
                            pe.wait_ge(fast_dve[k], at(FAST_DVE, t, "alpha", u))
                        else:
                            pe.wait_ge(fast_act[k], at(FAST_ACT, t, "agg", u))
                        width = D + 1 if l < 2 else D
                        for b in range(NB):
                            if l == 3:
                                last = nc.tensor.matmul(ps[u][:, b * D:(b + 1) * D], aggT[u][:, b * P:(b + 1) * P], w3[:, 0, :], start=True, stop=True)
                                continue
                            for c in range(NB):
                                last = nc.tensor.matmul(ps[u][:, b * width:(b + 1) * width], wgt[u][:, c, b * P:(b + 1) * P],
                                                        (vals if l < 2 else xs)[u][:, c, :], start=c == 0, stop=c == NB - 1)
                        last.then_inc(fast_pe[k], 1)

                steps = {"mask": transposed_mask, "transpose": transposes, "project": projections, "spread_d": spread_d,
                         "spread_s": spread_s, "score": scores, "gather": gather, "output": outputs}
                for step, l, k in order("pe"):
                    steps[step](l, k)

            pe.wait_ge(bad_step, 3)
            nc.tensor.matmul(ps[0][0:1, 0:1], bad[:, 8:9], ones_col[:, :], start=True, stop=True).then_inc(bad_summed, 1)

            def transpose_x(g, l):
                if l:
                    pe.wait_ge(gen_dve, done(GEN_DVE, g, f"norm{l - 1}"))
                for b in range(NB):
                    last = nc.tensor.transpose(ps_xT[:, b * P:(b + 1) * P], xg[:, b, :], ident[:, :])
                last.then_inc(gen_pe, 1)
                pe.wait_ge(gen_act, done(GEN_ACT, g, f"xT{l}"))

            def aggregate(values):
                for b in range(NB):
                    for c in range(NB):
                        last = nc.tensor.matmul(ps_o[:, b, :], prT[:, c, b * P:(b + 1) * P], values[:, c, 0:D],
                                                start=c == 0, stop=c == NB - 1)
                last.then_inc(gen_pe, 1)

            pe.wait_ge(redo_set, 1)
            with pe.If(pe.value_load(redo_i[0:1, 0:1], min_val=0, max_val=1)):
                with pe.Fori(0, B) as g:
                    pe.wait_ge(gen_in, g * 32 + 32)
                    pe.wait_ge(gen_dve, done(GEN_DVE, g, "adj"))
                    for c in range(NB):
                        for b in range(NB):
                            last = nc.tensor.transpose(ps_adjT[:, c, b * P:(b + 1) * P], adj_bf[:, b, c * P:(c + 1) * P], ident_bf[:, :])
                    last.then_inc(gen_pe, 1)
                    for l in range(2):
                        transpose_x(g, l)
                        for b in range(NB):
                            last = nc.tensor.matmul(ps_h[:, b * HC:(b + 1) * HC], xT[:, b * P:(b + 1) * P], w_ext[:, l, :],
                                                    start=True, stop=True)
                        last.then_inc(gen_pe, 1)
                        nc.tensor.matmul(ps_d[:, 0:N], wd_rep[:, l, :], xT[:, :], start=True, stop=True).then_inc(gen_pe, 1)
                        pe.wait_ge(gen_act, done(GEN_ACT, g, f"exp{l}"))
                        for c in range(NB):
                            for b in range(NB):
                                last = nc.tensor.transpose(ps_p[:, c, b * P:(b + 1) * P], pr[:, b, c * P:(c + 1) * P], ident[:, :])
                        last.then_inc(gen_pe, 1)
                        pe.wait_ge(gen_act, done(GEN_ACT, g, f"pT{l}"))
                        aggregate(h)
                    transpose_x(g, 2)
                    pe.wait_ge(gen_dve, done(GEN_DVE, g, "xTa"))
                    for r in range(R):
                        if r:
                            pe.wait_ge(gen_act, done(GEN_ACT, g, f"score{r - 1}"))
                        for c in range(NB):
                            last = nc.tensor.matmul(ps_p[:, c, :], xTa[:, r, c * P:(c + 1) * P], xT[:, :], start=True, stop=True)
                        last.then_inc(gen_pe, 1)
                    pe.wait_ge(gen_dve, done(GEN_DVE, g, "sum3"))
                    aggregate(xg)
                    transpose_x(g, 3)
                    for b in range(NB):
                        last = nc.tensor.matmul(ps_xw[:, b, :], xT[:, b * P:(b + 1) * P], w3[:, :, :].rearrange("p r d -> p (r d)"),
                                                start=True, stop=True)
                    last.then_inc(gen_pe, 1)
                    pe.wait_ge(gen_act, done(GEN_ACT, g, "xw"))
                    pe.wait_ge(gen_dve, done(GEN_DVE, g, "rel3"))
                    for b in range(NB):
                        for r in range(R):
                            for c in range(NB):
                                last = nc.tensor.matmul(ps_o[:, b, :], rel[:, r, c, b * P:(b + 1) * P], xw[:, c, r * D:(r + 1) * D],
                                                        start=r == 0 and c == 0, stop=r == R - 1 and c == NB - 1)
                    last.then_inc(gen_pe, 1)

_INS = ["x", "adj", "L0_gnn_W", "L0_gnn_a_src", "L0_gnn_a_dst", "L1_gnn_W", "L1_gnn_a", "L2_gnn_a0", "L2_gnn_a1",
        "L2_gnn_a2", "L2_gnn_a3", "L2_gnn_bias", "L3_gnn_adj", "L3_gnn_weight", "L3_gnn_bias"]


def kernel(**inputs):
    import numpy as np
    import concourse.bacc as bacc
    from concourse.bass_utils import run_bass_kernel_spmd

    nc = bacc.Bacc("TRN2", target_bir_lowering=False, num_devices=1)
    arrays, args = {}, []
    for name in _INS:
        a = np.ascontiguousarray(inputs[name])
        arrays[f"in_{name}"] = a
        args.append(nc.dram_tensor(f"in_{name}", a.shape, mybir.dt.from_np(a.dtype), kind="ExternalInput").ap())
    shape = np.shape(inputs["x"])
    args.append(nc.dram_tensor("out", shape, F32, kind="ExternalOutput").ap())
    res_gnn_kernel(nc, *args)
    r = run_bass_kernel_spmd(nc, [arrays], core_ids=[0])
    return r.results[0]["out"]
```
